# Optimizing a Trainium2 kernel written in Bass

```python
import numpy as np
import jax
import jax.numpy as jnp

def _softmax(x, axis=-1):
    return jax.nn.softmax(x, axis=axis)

def _gelu(x):
    return jax.nn.gelu(x, approximate=True)

def _silu(x):
    return jax.nn.silu(x)

def _sigmoid(x):
    return jax.nn.sigmoid(x)

def _layernorm(x, axis=-1, eps=1e-05):
    m = jnp.mean(x, axis=axis, keepdims=True)
    v = jnp.var(x, axis=axis, keepdims=True)
    return (x - m) / jnp.sqrt(v + eps)

def _scatter_add(tgt, idx, src, axis=0):
    return tgt.at[idx].add(src)

def _segment_sum(src, seg, n):
    return jax.ops.segment_sum(src, seg, n)
kernel_name = 'mk_xattn_ffn_d1_seqx_r2_4ff449'

def setup_inputs(seed: int=0):
    np.random.seed(seed)
    _w = jnp.asarray

    def _rec_inputs():
        import jax
        import jax.numpy as jnp
        _rk = jax.random.key(seed)
        x = -7.109e-05 + 0.9999 * jax.random.normal(jax.random.fold_in(_rk, 1), (4, 1024, 1024), jnp.float32)
        _lenS = 1024 - jax.random.randint(jax.random.fold_in(_rk, 7), (4,), 0, max(1, 1024 // 4) + 1, jnp.int32)
        _lenS2 = 1024 - jax.random.randint(jax.random.fold_in(_rk, 8), (4,), 0, max(1, 1024 // 4) + 1, jnp.int32)
        _ctx_2048P = jax.random.normal(jax.random.fold_in(_rk, 11), (4, 16, 1024), jnp.float32)
        _ctx_2048c = jax.random.dirichlet(jax.random.fold_in(_rk, 511), 0.3 * jnp.ones((16,), jnp.float32), (4, 1024))
        _ctx_2048t = jnp.einsum('bsk,bkd->bsd', _ctx_2048c, _ctx_2048P)
        _ctx_2048t = _ctx_2048t * jax.lax.rsqrt(jnp.mean(jnp.square(_ctx_2048t)) + 1e-12) * 0.953939
        ctx_2048 = -3.05549e-07 + 0.0199987 * (_ctx_2048t + 0.3 * jax.random.normal(jax.random.fold_in(_rk, 611), (4, 1024, 1024), jnp.float32))
        return (x, ctx_2048)
    x, ctx_2048 = _rec_inputs()

    def _L0_xattn_setup():
        import jax, jax.numpy as jnp
        import numpy as np
        FP8_MAX = 448.0
        ACT_EPS = 0.0001
        W_EPS = 1e-06
        BLK = 128

        def quant_dequant_act_1x128(x):
            E, M, K = x.shape
            xb = x.reshape(E, M, K // BLK, BLK)
            amax = jnp.max(jnp.abs(xb), axis=-1, keepdims=True)
            safe = jnp.maximum(amax, ACT_EPS)
            q = (xb * (FP8_MAX / safe)).astype(jnp.float8_e4m3fn)
            return (q.astype(jnp.float32) * (safe / FP8_MAX)).reshape(E, M, K)

        def quant_dequant_weight_128x128(w):
            E, N, K = w.shape
            wb = w.reshape(E, N // BLK, BLK, K // BLK, BLK)
            amax = jnp.max(jnp.abs(wb), axis=(2, 4), keepdims=True)
            safe = jnp.maximum(amax, W_EPS)
            q = (wb * (FP8_MAX / safe)).astype(jnp.float8_e4m3fn)
            return (q.astype(jnp.float32) * (safe / FP8_MAX)).reshape(E, N, K)
        key = jax.random.key(seed)
        kx, kw = jax.random.split(key)
        E, M, K, N = (8, 2048, 1024, 1024)
        x = jax.random.normal(kx, (E, M, K), dtype=jnp.float32)
        weight = jax.random.normal(kw, (E, N, K), dtype=jnp.float32) * 0.02
        return {'x': x, 'weight': weight}
    _L0_xattn_all = _L0_xattn_setup()
    _L0_xattn_in = {k: v for k, v in _L0_xattn_all.items() if k in ()}
    del _L0_xattn_all

    def _L0_ffn_setup():
        import jax, jax.numpy as jnp
        import numpy as np
        B, S, H = (2, 1024, 1024)
        E, G, TKG, K = (32, 8, 4, 8)
        I, SI = (512, 1024)
        ROUTED_SCALE = 2.5

        def _moe_forward(hidden_states, router_w, router_bias, w_gate, w_up, w_down, sw_gate, sw_up, sw_down):
            x = hidden_states.reshape(-1, H)
            T = x.shape[0]
            logits = x.astype(jnp.float32) @ router_w.astype(jnp.float32)
            scores = jax.nn.sigmoid(logits)
            scores_grouped = (scores + router_bias).reshape(T, G, E // G)
            top2, _ = jax.lax.top_k(scores_grouped, 2)
            group_scores = top2.sum(-1)
            _, top_groups = jax.lax.top_k(group_scores, TKG)
            mask = jnp.ones((T, G), bool).at[jnp.arange(T)[:, None], top_groups].set(False)
            masked = jnp.where(mask[:, :, None], 0.0, scores_grouped).reshape(T, E)
            _, top_k_index = jax.lax.top_k(masked, K)
            tkw = jnp.take_along_axis(scores, top_k_index, axis=-1)
            tkw = tkw / tkw.sum(-1, keepdims=True)
            tkw = (tkw * ROUTED_SCALE).astype(hidden_states.dtype)
            flat_idx = top_k_index.reshape(-1)
            sort_idx = jnp.argsort(flat_idx)
            xs = jnp.repeat(x, K, axis=0)[sort_idx]
            group_sizes = jnp.bincount(flat_idx, length=E).astype(jnp.int32)
            gate = jax.lax.ragged_dot(xs, w_gate, group_sizes)
            up = jax.lax.ragged_dot(xs, w_up, group_sizes)
            down = jax.lax.ragged_dot(jax.nn.silu(gate) * up, w_down, group_sizes)
            unsort = jnp.argsort(sort_idx)
            routed = (down[unsort].reshape(T, K, H) * tkw[..., None]).sum(axis=1)
            shared = jax.nn.silu(x @ sw_gate) * (x @ sw_up) @ sw_down
            return (routed + shared).reshape(hidden_states.shape)
        key = jax.random.key(seed)
        ks = jax.random.split(key, 9)

        def w(k, shape, fan_in):
            return jax.random.normal(k, shape, jnp.float32) / np.float32(np.sqrt(fan_in))
        return dict(hidden_states=jax.random.normal(ks[0], (B, S, H), jnp.float32), router_w=w(ks[1], (H, E), H), router_bias=jnp.zeros((E,), jnp.float32), w_gate=w(ks[2], (E, H, I), H), w_up=w(ks[3], (E, H, I), H), w_down=w(ks[4], (E, I, H), I), sw_gate=w(ks[5], (H, SI), H), sw_up=w(ks[6], (H, SI), H), sw_down=w(ks[7], (SI, H), SI))
    _L0_ffn_all = _L0_ffn_setup()
    _L0_ffn_in = {k: v for k, v in _L0_ffn_all.items() if k in ('router_w', 'router_bias', 'w_gate', 'w_up', 'w_down', 'sw_gate', 'sw_up', 'sw_down')}
    del _L0_ffn_all
    return {'x': x, 'ctx_2048': ctx_2048, 'L0_ffn_router_w': _L0_ffn_in['router_w'], 'L0_ffn_router_bias': _L0_ffn_in['router_bias'], 'L0_ffn_w_gate': _L0_ffn_in['w_gate'], 'L0_ffn_w_up': _L0_ffn_in['w_up'], 'L0_ffn_w_down': _L0_ffn_in['w_down'], 'L0_ffn_sw_gate': _L0_ffn_in['sw_gate'], 'L0_ffn_sw_up': _L0_ffn_in['sw_up'], 'L0_ffn_sw_down': _L0_ffn_in['sw_down']}

def reference(x, ctx_2048, L0_ffn_router_w, L0_ffn_router_bias, L0_ffn_w_gate, L0_ffn_w_up, L0_ffn_w_down, L0_ffn_sw_gate, L0_ffn_sw_up, L0_ffn_sw_down):
    import jax
    import jax.numpy as jnp

    def _L0_xattn_ref(x, weight):
        import jax, jax.numpy as jnp
        import numpy as np
        FP8_MAX = 448.0
        ACT_EPS = 0.0001
        W_EPS = 1e-06
        BLK = 128

        def quant_dequant_act_1x128(x):
            E, M, K = x.shape
            xb = x.reshape(E, M, K // BLK, BLK)
            amax = jnp.max(jnp.abs(xb), axis=-1, keepdims=True)
            safe = jnp.maximum(amax, ACT_EPS)
            q = (xb * (FP8_MAX / safe)).astype(jnp.float8_e4m3fn)
            return (q.astype(jnp.float32) * (safe / FP8_MAX)).reshape(E, M, K)

        def quant_dequant_weight_128x128(w):
            E, N, K = w.shape
            wb = w.reshape(E, N // BLK, BLK, K // BLK, BLK)
            amax = jnp.max(jnp.abs(wb), axis=(2, 4), keepdims=True)
            safe = jnp.maximum(amax, W_EPS)
            q = (wb * (FP8_MAX / safe)).astype(jnp.float8_e4m3fn)
            return (q.astype(jnp.float32) * (safe / FP8_MAX)).reshape(E, N, K)
        xq = quant_dequant_act_1x128(x)
        wq = quant_dequant_weight_128x128(weight)
        return jnp.einsum('emk,enk->emn', xq, wq)

    def _L0_ffn_ref(hidden_states, router_w, router_bias, w_gate, w_up, w_down, sw_gate, sw_up, sw_down):
        import jax, jax.numpy as jnp
        import numpy as np
        B, S, H = (2, 1024, 1024)
        E, G, TKG, K = (32, 8, 4, 8)
        I, SI = (512, 1024)
        ROUTED_SCALE = 2.5

        def _moe_forward(hidden_states, router_w, router_bias, w_gate, w_up, w_down, sw_gate, sw_up, sw_down):
            x = hidden_states.reshape(-1, H)
            T = x.shape[0]
            logits = x.astype(jnp.float32) @ router_w.astype(jnp.float32)
            scores = jax.nn.sigmoid(logits)
            scores_grouped = (scores + router_bias).reshape(T, G, E // G)
            top2, _ = jax.lax.top_k(scores_grouped, 2)
            group_scores = top2.sum(-1)
            _, top_groups = jax.lax.top_k(group_scores, TKG)
            mask = jnp.ones((T, G), bool).at[jnp.arange(T)[:, None], top_groups].set(False)
            masked = jnp.where(mask[:, :, None], 0.0, scores_grouped).reshape(T, E)
            _, top_k_index = jax.lax.top_k(masked, K)
            tkw = jnp.take_along_axis(scores, top_k_index, axis=-1)
            tkw = tkw / tkw.sum(-1, keepdims=True)
            tkw = (tkw * ROUTED_SCALE).astype(hidden_states.dtype)
            flat_idx = top_k_index.reshape(-1)
            sort_idx = jnp.argsort(flat_idx)
            xs = jnp.repeat(x, K, axis=0)[sort_idx]
            group_sizes = jnp.bincount(flat_idx, length=E).astype(jnp.int32)
            gate = jax.lax.ragged_dot(xs, w_gate, group_sizes)
            up = jax.lax.ragged_dot(xs, w_up, group_sizes)
            down = jax.lax.ragged_dot(jax.nn.silu(gate) * up, w_down, group_sizes)
            unsort = jnp.argsort(sort_idx)
            routed = (down[unsort].reshape(T, K, H) * tkw[..., None]).sum(axis=1)
            shared = jax.nn.silu(x @ sw_gate) * (x @ sw_up) @ sw_down
            return (routed + shared).reshape(hidden_states.shape)
        return _moe_forward(hidden_states, router_w, router_bias, w_gate, w_up, w_down, sw_gate, sw_up, sw_down)
    x = x + _L0_xattn_ref(_layernorm(x, axis=-1), ctx_2048)
    x = x + _L0_ffn_ref(_layernorm(x, axis=-1), L0_ffn_router_w, L0_ffn_router_bias, L0_ffn_w_gate, L0_ffn_w_up, L0_ffn_w_down, L0_ffn_sw_gate, L0_ffn_sw_up, L0_ffn_sw_down)
    return x

_drawn_inputs = setup_inputs


def setup_inputs(seed=0):
    import zlib

    import numpy as np

    out = dict(_drawn_inputs(seed))
    spreads = {'L0_ffn_router_bias': (0.0, 0.1)}
    factors = {}
    for name, (base, spread) in spreads.items():
        noise = np.random.default_rng([zlib.crc32(name.encode()), seed]).standard_normal(out[name].shape)
        drawn = base * np.exp(spread * noise) if base else spread * noise
        out[name] = jnp.asarray(drawn.astype(out[name].dtype))
    for name, factor in factors.items():
        out[name] = (out[name] * factor).astype(out[name].dtype)
    return out
```

```python
import concourse.bass as bass
from concourse import mybir
from contextlib import ExitStack

F32 = mybir.dt.float32
F32R = mybir.dt.float32r
BF16 = mybir.dt.bfloat16
I32 = mybir.dt.int32
U32 = mybir.dt.uint32
ALU = mybir.AluOpType
ACT = mybir.ActivationFunctionType
AX_X = mybir.AxisListType.X
RMAX = bass.bass_isa.ReduceOp.max

P = 128
B, S, H = 4, 1024, 1024
T = B * S
TT = T // P
BT = S // P
KB = H // P
E, G, TOPG, TOPK = 32, 8, 4, 8
EG = E // G
I = 512
IB = I // P
SH = 2
LN_EPS, ACT_EPS, W_EPS, FP8_MAX = 1e-5, 1e-4, 1e-6, 448.0
ROUTED_SCALE = 2.5
SHT = SH * TT
RT = (T * TOPK + (P - 1) * E) // P + 1
NT = SHT + RT
LT = NT + 3
NE = SH + E
CH = KB * I
MT = 3 * P
MAGIC = 1.5 * 2.0 ** 23
LOG2E, LN2_HI, LN2_LO = 1.4426950408889634, 0.693145751953125, 1.42860677e-06
EXP_C = [1.0, 1 / 2, 1 / 6, 1 / 24, 1 / 120, 1 / 720, 1 / 5040]
TAKEN = -3.0e38
assert NT % 2 == 0 and NT <= MT - 1 and IB * H == CH


def xattn_moe_program(nc, x, ctx_in, router_w, router_b, w_gate, w_up, w_down, sw_gate, sw_up, sw_down, out):
    x_rows = x.rearrange("b s h -> (b s) h")
    ctx_rows = ctx_in.rearrange("b s h -> (b s) h")
    tokens = nc.dram_tensor("tokens", [T + P, H], F32, kind="Internal").ap()
    slots = nc.dram_tensor("slots", [P * LT, 2], I32, kind="Internal").ap()
    tile_sets = nc.dram_tensor("tile_sets", [2, MT], I32, kind="Internal").ap()

    with ExitStack() as stack:
        def sb(name, shape, dt=F32):
            return stack.enter_context(nc.sbuf_tensor(name, shape, dt))

        def sem(name):
            return stack.enter_context(nc.semaphore(name))

        w_hi = sb("w_hi", [P, 3, CH], F32R)
        w_lo = sb("w_lo", [P, 3, CH], F32R)
        w_raw = sb("w_raw", [P, 3, CH])
        xT_hi = sb("xT_hi", [P, KB, P], F32R)
        xT_lo = sb("xT_lo", [P, KB, P], F32R)
        hT_hi = sb("hT_hi", [P, IB, P], F32R)
        hT_lo = sb("hT_lo", [P, IB, P], F32R)
        row_in = sb("row_in", [P, 2, H])
        row_out = sb("row_out", [P, 2, H])
        row_in_t = [row_in[:, n, :] for n in range(2)]
        row_out_t = [row_out[:, n, :] for n in range(2)]
        scr = sb("scr", [P, 7, H])
        sel_e = sb("sel_e", [P, TT * E], BF16)
        ident = sb("ident", [P, P])
        tri = sb("tri", [P, P], BF16)
        ones = sb("ones", [P, P], BF16)
        rw = sb("rw", [P, KB, E])
        bias = sb("bias", [P, E])
        stats = sb("stats", [P, 2, 6])
        mv = sb("mv", [P, 2])
        sm = sb("sm", [P, 8])
        sd = sb("sd", [P, 1])
        amax = sb("amax", [P, KB])
        amax_all = sb("amax_all", [P, KB])
        qscale = sb("qscale", [P, 3, KB])
        ef = sb("ef", [P, 8, E])
        ei = sb("ei", [P, E], I32)
        pick = sb("pick", [P, 2, E])
        top8 = sb("top8", [P, 8])
        token_no = sb("token_no", [P, TT], I32)
        tile_no = sb("tile_no", [P, 3], I32)
        tile_f = sb("tile_f", [P, 2, 3])
        tile_c = sb("tile_c", [P, 3, 3])
        set_i = sb("set_i", [P, 2, 3], I32)
        stage_rows = sb("stage_rows", [P, TOPK], I32)
        stage_picks = sb("stage_picks", [P, 2 * TOPK], I32)
        idx_g = [sb(f"idx_g{n}", [P, 2], I32) for n in range(2)]
        idx_s = [sb(f"idx_s{n}", [P, 2], I32) for n in range(2)]
        bank = [stack.enter_context(nc.psum_tensor(f"bank{n}", [P, 512], F32)) for n in range(8)]

        s_const = sem("s_const")
        s_init = sem("s_init")
        s_rw = sem("s_rw")
        s_row = [sem("s_row0"), sem("s_row1")]
        s_var = [sem("s_var0"), sem("s_var1")]
        s_sqrt = [sem("s_sqrt0"), sem("s_sqrt1")]
        s_amax = sem("s_amax")
        s_amax_all = sem("s_amax_all")
        s_quant = sem("s_quant")
        s_qT = sem("s_qT")
        s_qhi = sem("s_qhi")
        s_qlo = sem("s_qlo")
        s_prod = sem("s_prod")
        s_x1 = sem("s_x1")
        s_x1_st = [sem("s_x1_st0"), sem("s_x1_st1")]
        s_norm = sem("s_norm")
        s_norm_st = sem("s_norm_st")
        s_nT = sem("s_nT")
        s_nTs = sem("s_nTs")
        s_logit = sem("s_logit")
        s_logit_s = sem("s_logit_s")
        s_dve = sem("s_dve")
        s_passed = sem("s_passed")
        s_dve_ctx = sem("s_dve_ctx")
        s_dve_q = sem("s_dve_q")
        s_dve_p = sem("s_dve_p")
        s_sel = sem("s_sel")
        s_count = sem("s_count")
        s_slots = sem("s_slots")
        s_sets = sem("s_sets")
        s_meta_st = sem("s_meta_st")
        s_meta = sem("s_meta")
        s_stage = sem("s_stage")
        s_slot_st = sem("s_slot_st")
        s_raw = [sem(f"s_raw{c}") for c in range(3)]
        s_whi = sem("s_whi")
        s_wlo = sem("s_wlo")
        s_idx_g = [sem("s_idx_g0"), sem("s_idx_g1")]
        s_idx_s = [sem("s_idx_s0"), sem("s_idx_s1")]
        s_gath = [sem("s_gath0"), sem("s_gath1")]
        s_add = [sem("s_add0"), sem("s_add1")]
        s_xT = sem("s_xT")
        s_xhi = sem("s_xhi")
        s_xlo = sem("s_xlo")
        s_gate = sem("s_gate")
        s_up = sem("s_up")
        s_silu = sem("s_silu")
        s_h = sem("s_h")
        s_hT = sem("s_hT")
        s_hhi = sem("s_hhi")
        s_hlo = sem("s_hlo")
        s_down = sem("s_down")
        s_y = sem("s_y")

        block = stack.enter_context(nc.Block())
        v3 = lambda ap, a, b: ap.rearrange("p (a b) -> p a b", a=a, b=b)
        ctxT_hi = w_hi.rearrange("p c n -> p (c n)")[:, 0:KB * S].rearrange("p (k n) -> p k n", k=KB)
        ctxT_lo = w_lo.rearrange("p c n -> p (c n)")[:, 0:KB * S].rearrange("p (k n) -> p k n", k=KB)
        wide = lambda n: scr[:, n, :]
        NP = TT * TOPK
        slot_f = scr[:, 4, 0:NP].rearrange("p (i k) -> p i k", k=TOPK)
        slot_rows = scr[:, 4, NP:2 * NP].bitcast(I32)
        picks = scr[:, 4, 2 * NP:4 * NP].bitcast(I32).rearrange("p (n two) -> p n two", two=2)
        slot_i = scr[:, 0, 0:2 * NP].bitcast(I32).rearrange("p (a n) -> p a n", a=2)
        tile_row = scr[0:1, 1, 0:2 * MT].bitcast(I32).rearrange("o (d m) -> o d m", d=2)
        silu, hid = scr[:, 0, 0:I], scr[:, 0, I:2 * I]

        def token_tiles(eng, first, second):
            first(0, 0)
            with eng.Fori(0, BT // 2 - 1) as j:
                first(j, 1)
                second(j, 0)
                first(j, 2)
                second(j, 1)
            first(BT // 2 - 1, 1)
            second(BT // 2 - 1, 0)
            second(BT // 2 - 1, 1)

        @block.sync
        def _(sp):
            sp.dma_start(rw[:], router_w.rearrange("(k p) e -> p k e", p=P)).then_inc(s_rw, 16)
            sp.dma_start(bias[:], router_b.partition_broadcast(P)).then_inc(s_rw, 16)
            with sp.Fori(0, B) as b:
                def load(rows, j, off):
                    sp.dma_start(row_in_t[off % 2], rows[bass.ds(b * S + j * (2 * P) + off * P, P), :]).then_inc(s_row[off % 2], 16)

                sp.wait_ge(s_x1, b * BT)
                for n in range(2):
                    load(ctx_rows, 0, n)
                with sp.Fori(0, BT // 2 - 1) as j:
                    for n in range(2):
                        sp.wait_ge(s_quant, b * (2 * BT) + j * 2 + (n + 1))
                        load(ctx_rows, j, 2 + n)
                for n in range(2):
                    sp.wait_ge(s_quant, b * (2 * BT) + (BT - 1 + n))
                    load(x_rows, 0, n)
                with sp.Fori(0, BT // 2 - 1) as j:
                    for n in range(2):
                        sp.wait_ge(s_x1, b * BT + j * 2 + (n + 1))
                        load(x_rows, j, 2 + n)

            def chunk(c, s):
                return w_raw[:, c, :].rearrange("p (k n) -> p k n", n=s)

            for s in range(SH):
                for c, src in enumerate((sw_gate, sw_up, sw_down)):
                    if s > 0:
                        sp.wait_ge(s_wlo, 3 * (s - 1) + c + 1)
                    if c < 2:
                        sp.dma_start(chunk(c, I), src[:, s * I:(s + 1) * I].rearrange("(k p) n -> p k n", p=P)).then_inc(s_raw[c], 16)
                    else:
                        sp.dma_start(chunk(c, H), src[s * I:(s + 1) * I, :].rearrange("(k p) n -> p k n", p=P)).then_inc(s_raw[c], 16)
            with sp.Fori(0, E) as e:
                for c, src in enumerate((w_gate, w_up, w_down)):
                    sp.wait_ge(s_wlo, e * 3 + (3 * (SH - 1) + c + 1))
                    rows = src.rearrange("e k n -> (e k) n")[bass.ds(e * src.shape[1], src.shape[1]), :]
                    sp.dma_start(chunk(c, src.shape[2]), rows.rearrange("(k p) n -> p k n", p=P)).then_inc(s_raw[c], 16)

        @block.gpsimd
        def _(pool):
            pool.memset(ident[:], 0.0).then_inc(s_const, 1)
            pool.memset(tri[:], 1.0).then_inc(s_const, 1)
            pool.memset(ones[:], 1.0).then_inc(s_const, 1)
            pool.memset(wide(6), 0.0).then_inc(s_const, 1)
            table = scr[:, 4, 0:2 * LT].bitcast(I32).rearrange("p (t two) -> p t two", two=2)
            weight = scr[:, 4, 0:2 * LT].rearrange("p (t two) -> p t two", two=2)
            pool.iota(table[:, 0:SHT, 0:1], [[0, SH], [P, TT], [0, 1]], base=0, channel_multiplier=1).then_inc(s_const, 1)
            pool.iota(table[:, SHT:LT, 0:1], [[0, LT - SHT], [0, 1]], base=T, channel_multiplier=1).then_inc(s_const, 1)
            pool.memset(weight[:, 0:SHT, 1:2], 1.0).then_inc(s_const, 1)
            pool.memset(weight[:, SHT:LT, 1:2], 0.0).then_inc(s_const, 1)
            pool.iota(token_no[:], [[P, TT]], base=0, channel_multiplier=1).then_inc(s_const, 1)
            pool.iota(tile_no[:], [[P, 3]], base=0, channel_multiplier=1).then_inc(s_const, 1)
            pool.wait_ge(s_const, 10)
            pool.affine_select(out=ident[:], in_=ident[:], compare_op=ALU.not_equal, fill=1.0,
                               base=0, pattern=[[-1, P]], channel_multiplier=1).then_inc(s_const, 1)
            pool.affine_select(out=tri[:], in_=tri[:], compare_op=ALU.is_gt, fill=0.0,
                               base=0, pattern=[[1, P]], channel_multiplier=-1).then_inc(s_const, 1)
            pool.dma_start(slots.rearrange("(p t) two -> p (t two)", p=P), scr[:, 4, 0:2 * LT].bitcast(I32)).then_inc(s_init, 16)
            pool.dma_start(tokens[T:T + P, :], wide(6)).then_inc(s_init, 16)
            pool.dma_start(out[T:T + P, :], wide(6)).then_inc(s_init, 16)
            pool.wait_ge(s_init, 48)

            with pool.Fori(0, B) as b:
                with pool.Fori(0, BT) as j:
                    pool.wait_ge(s_amax, b * BT + j + 1)
                    pool.sem_inc(s_passed)
                    pool.partition_all_reduce(amax_all[:], amax[:], P, RMAX).then_inc(s_amax_all, 1)
                with pool.Fori(0, BT // 2) as j:
                    for n in range(2):
                        rows = bass.ds(b * S + j * (2 * P) + n * P, P)
                        pool.wait_ge(s_x1, b * BT + j * 2 + n + 1)
                        pool.sem_inc(s_passed)
                        pool.dma_start(out[rows, :], row_out_t[n]).then_inc(s_x1_st[n], 16)
                        pool.wait_ge(s_norm, b * BT + j * 2 + n + 1)
                        pool.sem_inc(s_passed)
                        pool.dma_start(tokens[rows, :], wide(3)).then_inc(s_norm_st, 16)
            for n in range(2):
                pool.wait_ge(s_x1_st[n], 16 * (TT // 2))
            pool.wait_ge(s_norm_st, 16 * TT)

            slot_tiles = slots.rearrange("(p t) two -> p t two", p=P)

            def load_idx(dst, t, done):
                pool.dma_start(dst[:], slot_tiles[:, bass.ds(t, 1), :].rearrange("p t two -> p (t two)")).then_inc(done, 16)

            def gather(n):
                pool.indirect_dma_start(out=row_in_t[n], out_offset=None, in_=tokens[:, :],
                                        in_offset=bass.IndirectOffsetOnAxis(ap=idx_g[n][:, 0:1].bitcast(U32), axis=0)).then_inc(s_gath[n], 16)

            def tile_step(it, n):
                pool.wait_ge(s_idx_g[n], it * 16 + 32)
                pool.wait_ge(s_xT, it * 4 + (2 * n + 2))
                pool.sem_inc(s_passed)
                gather(n)
                pool.wait_ge(s_gath[1 - n], it * 16 + (16 + 16 * n))
                pool.sem_inc(s_passed)
                if n == 0:
                    load_idx(idx_g[1], it * 2 + 3, s_idx_g[1])
                else:
                    load_idx(idx_g[0], it * 2 + 4, s_idx_g[0])
                pool.wait_ge(s_y, it * 4 + (2 * n + 2))
                if n == 0:
                    pool.wait_ge(s_add[1], it * 16)
                else:
                    pool.wait_ge(s_add[0], it * 16 + 16)
                pool.sem_inc(s_passed)
                pool.indirect_dma_start(out=out[:, :], out_offset=bass.IndirectOffsetOnAxis(ap=idx_s[n][:, 0:1].bitcast(U32), axis=0),
                                        in_=row_out_t[n], in_offset=None, compute_op=ALU.add).then_inc(s_add[n], 16)
                pool.wait_ge(s_add[n], it * 16 + 16)
                pool.sem_inc(s_passed)
                load_idx(idx_s[n], it * 2 + (n + 2), s_idx_s[n])

            for n in range(2):
                load_idx(idx_g[n], n, s_idx_g[n])
                load_idx(idx_s[n], n, s_idx_s[n])
            for n in range(2):
                pool.wait_ge(s_idx_g[n], 16)
                gather(n)
            pool.wait_ge(s_gath[0], 16)
            load_idx(idx_g[0], 2, s_idx_g[0])

            pool.wait_ge(s_sets, 1)
            for d in range(2):
                with nc.allow_non_contiguous_dma(reason="three values per partition"):
                    pool.dma_start(tile_sets[d:d + 1, :].rearrange("a (c p) -> p (a c)", p=P), set_i[:, d, :]).then_inc(s_meta_st, 16)
            pool.wait_ge(s_meta_st, 32)
            pool.dma_start(tile_row, tile_sets[:, :].rearrange("(o d) m -> o d m", o=1)).then_inc(s_meta, 16)

            pool.wait_ge(s_slots, 1)
            pool.wait_ge(s_init, 48)
            last_shared = SHT // 2 - 2
            with pool.Fori(0, TT) as i:
                pool.wait_ge(s_slot_st, i * (16 * TOPK))
                pool.tensor_copy(stage_rows[:], slot_rows[:, bass.ds(i * TOPK, TOPK)]).then_inc(s_stage, 1)
                pool.tensor_copy(stage_picks[:], picks.rearrange("p n two -> p (n two)")[:, bass.ds(i * (2 * TOPK), 2 * TOPK)]).then_inc(s_stage, 1)
                pool.wait_ge(s_stage, i * 2 + 2)
                pool.sem_inc(s_passed)
                for k in range(TOPK):
                    pool.indirect_dma_start(out=slots[:, :], out_offset=bass.IndirectOffsetOnAxis(ap=stage_rows[:, k:k + 1].bitcast(U32), axis=0),
                                            in_=stage_picks[:, 2 * k:2 * k + 2], in_offset=None).then_inc(s_slot_st, 16)
                with pool.If(i < last_shared):
                    for n in range(2):
                        tile_step(i, n)
            pool.wait_ge(s_slot_st, 16 * TOPK * TT)
            with pool.Fori(last_shared, NT // 2) as it:
                for n in range(2):
                    tile_step(it, n)
            for n in range(2):
                pool.wait_ge(s_add[n], 16 * (NT // 2))
                pool.wait_ge(s_idx_g[n], 16 * (NT // 2 + 1) + (16 if n == 0 else 0))
                pool.wait_ge(s_idx_s[n], 16 * (NT // 2 + 1))
                pool.wait_ge(s_gath[n], 16 * (NT // 2 + 1))

        @block.scalar
        def _(act):
            with act.Fori(0, B) as b:
                act.wait_ge(s_prod, b * BT)
                with act.Fori(0, BT) as j:
                    for c in range(2):
                        act.wait_ge(s_qT, b * (4 * BT) + j * 2 + (c + 1))
                        act.activation(ctxT_hi[:, 4 * c:4 * c + 4, bass.ds(j * P, P)], v3(bank[c][:], 4, P), ACT.Copy).then_inc(s_qhi, 1)

                def root(k, j, off):
                    act.wait_ge(s_var[k], b * BT + j * 2 + (off + 1))
                    act.activation(sd[:], sm[:, 0:1], ACT.Sqrt).then_inc(s_sqrt[k], 1)

                def first(j, off):
                    root(0, j, off)
                    act.wait_ge(s_prod, b * BT + j * 2 + off)
                    for c in range(2):
                        act.wait_ge(s_qT, b * (4 * BT) + j * 4 + (2 * BT + 2 * off + c + 1))
                        act.activation(xT_hi[:, 4 * c:4 * c + 4, :], v3(bank[c][:], 4, P), ACT.Copy).then_inc(s_qhi, 1)

                def second(j, off):
                    root(1, j, off)
                    act.wait_ge(s_logit, b * BT + j * 2 + off)
                    for c in range(2):
                        act.wait_ge(s_nT, b * (2 * BT) + j * 4 + (2 * off + c + 1))
                        act.activation(wide(5)[:, c * 512:(c + 1) * 512], bank[2 + c][:], ACT.Copy).then_inc(s_nTs, 1)
                    act.wait_ge(s_logit, b * BT + j * 2 + (off + 1))
                    act.activation(wide(6)[:, bass.ds(b * (BT * E) + j * (2 * E) + off * E, E)], bank[4][:, 0:E], ACT.Copy).then_inc(s_logit_s, 1)

                token_tiles(act, first, second)

            def split_hi(c, loaded):
                act.wait_ge(s_raw[c], loaded)
                act.activation(w_hi[:, c, :], w_raw[:, c, :], ACT.Copy).then_inc(s_whi, 1)

            def gathered_hi(k):
                for c in range(2):
                    act.wait_ge(s_xT, k * 2 + (c + 1))
                    act.activation(xT_hi[:, 4 * c:4 * c + 4, :], v3(bank[c][:], 4, P), ACT.Copy).then_inc(s_xhi, 1)

            act.wait_ge(s_prod, TT)
            for c in range(3):
                split_hi(c, 16)
            gathered_hi(0)
            act.wait_ge(s_meta, 16)
            with act.Fori(0, NT // 2) as it:
                for n in range(2):
                    t = it * 2 + n
                    act.wait_ge(s_gate, t + 1)
                    act.wait_ge(s_h, t * 2)
                    act.activation(silu[:], bank[2][:], ACT.Silu).then_inc(s_silu, 1)
                    for u in range(2):
                        act.wait_ge(s_hT, t * 2 + (u + 1))
                        act.activation(hT_hi[:, 2 * u:2 * u + 2, :], v3(bank[5][:, 0:256], 2, P), ACT.Copy).then_inc(s_hhi, 1)
                    act.wait_ge(s_up, t * 2 + 2)
                    gathered_hi(t + 1)
                    for c in range(2):
                        act.wait_ge(s_down, t * 2 + (c + 1))
                        if c == 0:
                            act.wait_ge(s_idx_s[n], it * 16 + 16)
                            if n == 0:
                                act.wait_ge(s_add[0], it * 16)
                            else:
                                act.wait_ge(s_add[1], it * 16)
                        act.activation(row_out_t[n][:, c * 512:(c + 1) * 512], bank[6 + c][:], ACT.Copy,
                                       scale=idx_s[n][:, 1:2].bitcast(F32)).then_inc(s_y, 1)
                    last = act.value_load(tile_row[0:1, 1, bass.ds(t, 1)], min_val=0, max_val=1)
                    set_no = act.value_load(tile_row[0:1, 0, bass.ds(t, 1)], min_val=0, max_val=NE - 1)
                    with act.If(last > 0):
                        for c in range(3):
                            split_hi(c, set_no * 16 + 32)

        @block.vector
        def _(v):
            chain = [None, 0, 0]

            def start(s, before):
                chain[:] = [s, before, 0]

            def link(ins):
                chain[2] += 1
                ins.then_inc(chain[0], 1)
                v.wait_ge(chain[0], chain[1] + chain[2])

            def moments(src, k):
                v.bn_stats(stats[:, 0, :], src[:, 0:512])
                link(v.bn_stats(stats[:, 1, :], src[:, 512:1024]))
                v.sem_inc(s_passed)
                link(v.bn_aggr(mv[:], stats.rearrange("p a b -> p (a b)")))
                v.tensor_scalar(sm[:, 0:1], mv[:, 1:2], LN_EPS, None, ALU.add).then_inc(s_var[k], 1)

            def inverse_root():
                link(v.reciprocal(sm[:, 1:2], sd[:]))
                link(v.scalar_tensor_tensor(sm[:, 2:3], sm[:, 1:2], sm[:, 0:1], sm[:, 1:2], ALU.mult, ALU.mult))
                link(v.tensor_scalar(sm[:, 3:4], sm[:, 2:3], -0.5, 1.5, ALU.mult, ALU.add))
                link(v.tensor_tensor(sm[:, 4:5], sm[:, 3:4], sm[:, 1:2], ALU.mult))

            def quantise(src, maxima, eps):
                link(v.tensor_scalar(qscale[:, 0, :], maxima, eps, None, ALU.max))
                link(v.reciprocal(qscale[:, 1, :], qscale[:, 0, :]))
                v.tensor_scalar(qscale[:, 1, :], qscale[:, 1, :], FP8_MAX, None, ALU.mult)
                link(v.tensor_scalar(qscale[:, 2, :], qscale[:, 0, :], 1.0 / FP8_MAX, None, ALU.mult))
                by = lambda n: qscale[:, n, :].unsqueeze(2).to_broadcast([P, KB, P])
                y, e = wide(1), wide(2)
                link(v.tensor_tensor(v3(y, KB, P), v3(src, KB, P), by(1), ALU.mult))
                link(v.tensor_scalar(e.bitcast(U32), y.bitcast(U32), 0x7F800000, None, ALU.bitwise_and))
                link(v.tensor_scalar(e, e, 2.0 ** -6, 1.5 * 2.0 ** 20, ALU.max, ALU.mult))
                link(v.tensor_tensor(y, y, e, ALU.add))
                link(v.tensor_tensor(y, y, e, ALU.subtract))
                v.tensor_tensor(v3(y, KB, P), v3(y, KB, P), by(2), ALU.mult).then_inc(s_quant, 1)

            v.wait_ge(s_const, 12)
            K_CTX, K_Q, K_P = 8, 16, 6
            with v.Fori(0, B) as b:
                with v.Fori(0, BT // 2) as j:
                    for n in range(2):
                        src = row_in_t[n]
                        start(s_dve_ctx, b * (BT * K_CTX) + j * (2 * K_CTX) + n * K_CTX)
                        v.wait_ge(s_row[n], b * (16 * BT) + j * 16 + 16)
                        v.tensor_reduce(amax[:], v3(src, KB, P), AX_X, ALU.max, apply_absolute_value=True).then_inc(s_amax, 1)
                        v.wait_ge(s_amax_all, b * BT + j * 2 + (n + 1))
                        v.wait_ge(s_qT, b * (4 * BT) + j * 4 + 2 * n)
                        quantise(src, amax_all[:], W_EPS)
                        for c in range(2):
                            v.wait_ge(s_qhi, b * (4 * BT) + j * 4 + (2 * n + c + 1))
                            at = bass.ds(j * (2 * P) + n * P, P)
                            v.tensor_tensor(ctxT_lo[:, 4 * c:4 * c + 4, at], v3(bank[c][:], 4, P),
                                            ctxT_hi[:, 4 * c:4 * c + 4, at].bitcast(F32), ALU.subtract).then_inc(s_qlo, 1)
                        assert chain[2] == K_CTX, chain

                def first(j, off):
                    src = row_in_t[off % 2]
                    start(s_dve_q, b * (BT * K_Q) + j * (2 * K_Q) + off * K_Q)
                    v.wait_ge(s_row[off % 2], b * (16 * BT) + j * 16 + (8 * BT + 16 * (off // 2 + 1)))
                    moments(src, 0)
                    v.wait_ge(s_sqrt[0], b * BT + j * 2 + (off + 1))
                    inverse_root()
                    link(v.tensor_scalar(wide(0), src, mv[:, 0:1], sm[:, 4:5], ALU.subtract, ALU.mult))
                    link(v.tensor_reduce(amax[:], v3(wide(0), KB, P), AX_X, ALU.max, apply_absolute_value=True))
                    v.wait_ge(s_qT, b * (4 * BT) + j * 4 + (2 * BT + 2 * off))
                    quantise(wide(0), amax[:], ACT_EPS)
                    for c in range(2):
                        v.wait_ge(s_qhi, b * (4 * BT) + j * 4 + (2 * BT + 2 * off + c + 1))
                        v.tensor_tensor(xT_lo[:, 4 * c:4 * c + 4, :], v3(bank[c][:], 4, P),
                                        xT_hi[:, 4 * c:4 * c + 4, :].bitcast(F32), ALU.subtract).then_inc(s_qlo, 1)
                    assert chain[2] == K_Q, chain

                def second(j, off):
                    n = off % 2
                    start(s_dve_p, b * (BT * K_P) + j * (2 * K_P) + off * K_P)
                    v.wait_ge(s_prod, b * BT + j * 2 + (off + 1))
                    v.wait_ge(s_x1_st[n], b * (8 * BT) + j * 16)
                    for c in range(2):
                        cols = slice(c * 512, (c + 1) * 512)
                        last = v.tensor_tensor(row_out_t[n][:, cols], bank[6 + c][:], row_in_t[n][:, cols], ALU.add)
                    last.then_inc(s_x1, 1)
                    v.wait_ge(s_x1, b * BT + j * 2 + (off + 1))
                    moments(row_out_t[n], 1)
                    v.wait_ge(s_sqrt[1], b * BT + j * 2 + (off + 1))
                    inverse_root()
                    v.wait_ge(s_norm_st, b * (16 * BT) + j * 32 + 16 * off)
                    v.wait_ge(s_nT, b * (2 * BT) + j * 4 + 2 * off)
                    v.tensor_scalar(wide(3), row_out_t[n], mv[:, 0:1], sm[:, 4:5], ALU.subtract, ALU.mult).then_inc(s_norm, 1)
                    assert chain[2] == K_P, chain

                token_tiles(v, first, second)

            def split_lo(c, done):
                v.wait_ge(s_whi, done)
                v.tensor_tensor(w_lo[:, c, :], w_raw[:, c, :], w_hi[:, c, :].bitcast(F32), ALU.subtract).then_inc(s_wlo, 1)

            for c in range(3):
                split_lo(c, c + 1)

            start(s_dve, 0)
            v.wait_ge(s_logit_s, TT)
            v.wait_ge(s_norm_st, 16 * TT)
            v.wait_ge(s_rw, 32)
            tte = lambda n: wide(n).rearrange("p (i e) -> p i e", e=E)
            link(v.tensor_scalar(wide(0), wide(6), -80.0, 80.0, ALU.max, ALU.min))
            link(v.tensor_scalar(wide(1), wide(0), -LOG2E, MAGIC, ALU.mult, ALU.add))
            link(v.tensor_scalar(wide(1), wide(1), MAGIC, None, ALU.subtract))
            link(v.scalar_tensor_tensor(wide(2), wide(1), -LN2_HI, wide(0), ALU.mult, ALU.subtract))
            link(v.scalar_tensor_tensor(wide(2), wide(1), -LN2_LO, wide(2), ALU.mult, ALU.add))
            link(v.tensor_scalar(wide(3), wide(2), EXP_C[-1], None, ALU.mult))
            for coef in EXP_C[-2::-1]:
                link(v.scalar_tensor_tensor(wide(3), wide(3), coef, wide(2), ALU.add, ALU.mult))
            link(v.tensor_scalar(wide(4).bitcast(I32), wide(1), 127.0, 2.0 ** 23, ALU.add, ALU.mult))
            link(v.scalar_tensor_tensor(wide(3), wide(3), 1.0, wide(4), ALU.add, ALU.mult))
            link(v.tensor_scalar(wide(3), wide(3), 1.0, None, ALU.add))
            link(v.reciprocal(wide(0), wide(3)))
            link(v.tensor_tensor(tte(1), tte(0), bias[:].unsqueeze(1).to_broadcast([P, TT, E]), ALU.add))
            four = wide(1).rearrange("p (q m) -> p q m", m=EG)
            col = lambda m: four[:, :, m]
            q4 = lambda n, m: wide(n)[:, 256 * m:256 * m + 256]
            v.tensor_tensor(q4(2, 0), col(0), col(1), ALU.max)
            v.tensor_tensor(q4(2, 1), col(0), col(1), ALU.min)
            v.tensor_tensor(q4(2, 2), col(2), col(3), ALU.max)
            link(v.tensor_tensor(q4(2, 3), col(2), col(3), ALU.min))
            v.tensor_tensor(q4(3, 0), q4(2, 0), q4(2, 2), ALU.max)
            v.tensor_tensor(q4(3, 1), q4(2, 0), q4(2, 2), ALU.min)
            link(v.tensor_tensor(q4(3, 2), q4(2, 1), q4(2, 3), ALU.max))
            link(v.tensor_tensor(q4(3, 1), q4(3, 1), q4(3, 2), ALU.max))
            link(v.tensor_tensor(q4(3, 3), q4(3, 0), q4(3, 1), ALU.add))
            gs = q4(3, 3).rearrange("p (i g) -> p i g", g=G)
            pairs = scr[:, 4:6, :].rearrange("p a (i g o) -> p (a i) g o", g=G, o=G)
            link(v.memset(scr[:, 4:6, :], 0.0))
            for o in range(G):
                if o > 0:
                    last = v.tensor_tensor(pairs[:, :, 0:o, o], gs[:, :, o].unsqueeze(2).to_broadcast([P, TT, o]), gs[:, :, 0:o], ALU.is_gt)
                if o < G - 1:
                    last = v.tensor_tensor(pairs[:, :, o + 1:G, o], gs[:, :, o].unsqueeze(2).to_broadcast([P, TT, G - 1 - o]), gs[:, :, o + 1:G], ALU.is_ge)
            link(last)
            link(v.tensor_reduce(q4(2, 0), pairs, AX_X, ALU.add))
            link(v.tensor_scalar(q4(2, 1), q4(2, 0), TOPG - 0.5, None, ALU.is_lt))
            keep = q4(2, 1).unsqueeze(2).to_broadcast([P, TT * G, EG])
            link(v.tensor_tensor(wide(3).rearrange("p (q m) -> p q m", m=EG), four, keep, ALU.mult))
            link(v.tensor_scalar(wide(3), wide(3), 0.0, None, ALU.add))
            before = chain[2]
            with v.Fori(0, TT) as i:
                start(s_dve, i * 4 + before)
                at = bass.ds(i * E, E)
                link(v.tensor_copy(pick[:, 0, :], wide(3)[:, at]))
                v.sem_inc(s_passed)
                link(v.max(top8[:], pick[:, 0, :]))
                v.sem_inc(s_passed)
                link(v.match_replace(pick[:, 1, :], top8[:], pick[:, 0, :], TAKEN))
                link(v.tensor_scalar(wide(4)[:, at], pick[:, 1, :], TAKEN, None, ALU.is_equal))
            start(s_dve, before + 4 * TT)
            v.tensor_copy(sel_e.rearrange("p (e i) -> p e i", i=TT), tte(4).rearrange("p i e -> p e i")).then_inc(s_sel, 1)
            link(v.tensor_tensor(wide(1), wide(0), wide(4), ALU.mult))
            link(v.tensor_reduce(ef[:, 0, :], tte(1), AX_X, ALU.add))
            link(v.reciprocal(ef[:, 1, :], ef[:, 0, :]))
            link(v.tensor_tensor(tte(1), tte(1), ef[:, 1, :].unsqueeze(2).to_broadcast([P, TT, E]), ALU.mult))
            link(v.tensor_scalar(wide(1), wide(1), ROUTED_SCALE, None, ALU.mult))
            link(v.memset(wide(3), 1.0))
            link(v.memset(tte(3)[:, :, 0:1], 0.0))
            v.wait_ge(s_count, 4)
            for c in range(2):
                last = v.tensor_copy(wide(2)[:, 512 * c:512 * c + 512], bank[2 + c][:])
            link(last)
            link(v.tensor_tensor_scan(wide(5), wide(3), wide(2), 0.0, ALU.mult, ALU.add))
            eti = lambda n: wide(n).rearrange("p (e i) -> p e i", i=TT)
            link(v.tensor_scalar(ei[:], eti(5)[:, :, TT - 1], float(P - 1), None, ALU.add))
            link(v.tensor_scalar(ei[:], ei[:], 7, None, ALU.logical_shift_right))
            link(v.tensor_scalar(ef[:, 2, :], ei[:], 1.0, None, ALU.max))
            link(v.memset(ef[:, 3, :], 1.0))
            link(v.tensor_tensor_scan(ef[:, 4, :], ef[:, 3, :], ef[:, 2, :], 0.0, ALU.mult, ALU.add))
            link(v.tensor_tensor(ef[:, 5, :], ef[:, 4, :], ef[:, 2, :], ALU.subtract))
            link(v.tensor_scalar(ef[:, 6, :], ef[:, 5, :], float(SHT), float(P), ALU.add, ALU.mult))
            link(v.tensor_scalar(ef[:, 7, :], ef[:, 4, :], float(SHT), None, ALU.add))
            link(v.tensor_tensor(wide(6), wide(5), wide(2), ALU.subtract))
            for c in range(2):
                last = v.tensor_tensor(wide(6)[:, 512 * c:512 * c + 512], bank[c][:], wide(6)[:, 512 * c:512 * c + 512], ALU.add)
            link(last)
            link(v.tensor_tensor(eti(6), eti(6), ef[:, 6, :].unsqueeze(2).to_broadcast([P, E, TT]), ALU.add))
            link(v.tensor_tensor_scan(wide(2), wide(3), wide(4), 0.0, ALU.mult, ALU.add))
            link(v.tensor_tensor(wide(2), wide(2), wide(4), ALU.mult))
            place = eti(6).rearrange("p e i -> p i e")
            picks_w = picks.bitcast(F32).rearrange("p (i k) two -> p i k two", k=TOPK)
            for k in range(TOPK):
                v.scalar_tensor_tensor(tte(3), tte(2), float(k + 1), place, ALU.is_equal, ALU.mult)
                link(v.scalar_tensor_tensor(tte(5), tte(2), float(k + 1), tte(1), ALU.is_equal, ALU.mult))
                v.tensor_reduce(slot_f[:, :, k], tte(3), AX_X, ALU.add)
                link(v.tensor_reduce(picks_w[:, :, k, 1], tte(5), AX_X, ALU.add))
            tok = token_no[:].unsqueeze(2).to_broadcast([P, TT, TOPK])
            v.tensor_copy(picks.rearrange("p (i k) two -> p i k two", k=TOPK)[:, :, :, 0], tok)
            link(v.tensor_copy(slot_i[:, 0, :], slot_f.rearrange("p i k -> p (i k)")))
            link(v.tensor_scalar(slot_i[:, 1, :], slot_i[:, 0, :], 7, None, ALU.logical_shift_right))
            link(v.tensor_scalar(slot_i[:, 0, :], slot_i[:, 0, :], P - 1, None, ALU.bitwise_and))
            v.scalar_tensor_tensor(slot_rows[:], slot_i[:, 0, :], float(LT), slot_i[:, 1, :], ALU.mult, ALU.add).then_inc(s_slots, 1)
            v.tensor_copy(tile_f[:, 0, :], tile_no[:])
            link(v.tensor_scalar(tile_f[:, 1, :], tile_no[:], 1.0, None, ALU.add))
            cmp = lambda d: wide(2 + d)[:, 0:3 * E].rearrange("p (c e) -> p c e", e=E)
            ends = ef[:, 7, :].unsqueeze(1).to_broadcast([P, 3, E])
            for d in range(2):
                link(v.tensor_tensor(cmp(d), tile_f[:, d, :].unsqueeze(2).to_broadcast([P, 3, E]), ends, ALU.is_ge))
                link(v.tensor_reduce(tile_c[:, d, :], cmp(d), AX_X, ALU.add))
                link(v.scalar_tensor_tensor(tile_c[:, d, :], tile_f[:, d, :], float(TT), tile_c[:, d, :], ALU.is_ge, ALU.add))
                link(v.scalar_tensor_tensor(tile_c[:, d, :], tile_f[:, d, :], float(SHT), tile_c[:, d, :], ALU.is_ge, ALU.add))
                link(v.tensor_scalar(tile_c[:, d, :], tile_c[:, d, :], float(NE - 1), None, ALU.min))
            v.tensor_copy(set_i[:, 0, :], tile_c[:, 0, :])
            v.tensor_tensor(set_i[:, 1, :], tile_c[:, 1, :], tile_c[:, 0, :], ALU.subtract).then_inc(s_sets, 1)

            def gathered_lo(k):
                for c in range(2):
                    v.wait_ge(s_xhi, k * 2 + (c + 1))
                    v.tensor_tensor(xT_lo[:, 4 * c:4 * c + 4, :], v3(bank[c][:], 4, P),
                                    xT_hi[:, 4 * c:4 * c + 4, :].bitcast(F32), ALU.subtract).then_inc(s_xlo, 1)

            gathered_lo(0)
            v.wait_ge(s_meta, 16)
            with v.Fori(0, NT // 2) as it:
                for n in range(2):
                    t = it * 2 + n
                    v.wait_ge(s_silu, t + 1)
                    for u in range(2):
                        cols = slice(256 * u, 256 * u + 256)
                        v.wait_ge(s_up, t * 2 + (u + 1))
                        v.tensor_tensor(hid[:, cols], bank[3 + u][:, 0:256], silu[:, cols], ALU.mult).then_inc(s_h, 1)
                        v.wait_ge(s_hhi, t * 2 + (u + 1))
                        v.tensor_tensor(hT_lo[:, 2 * u:2 * u + 2, :], v3(bank[5][:, 0:256], 2, P),
                                        hT_hi[:, 2 * u:2 * u + 2, :].bitcast(F32), ALU.subtract).then_inc(s_hlo, 1)
                    gathered_lo(t + 1)
                    last = v.value_load(tile_row[0:1, 1, bass.ds(t, 1)], min_val=0, max_val=1)
                    set_no = v.value_load(tile_row[0:1, 0, bass.ds(t, 1)], min_val=0, max_val=NE - 1)
                    with v.If(last > 0):
                        for c in range(3):
                            split_lo(c, set_no * 3 + (4 + c))

        @block.tensor
        def _(pe):
            def transposes(dst, src, c, done):
                for k in range(4):
                    last = pe.transpose(dst[:, k * P:(k + 1) * P], src[:, (4 * c + k) * P:(4 * c + k + 1) * P], ident[:])
                last.then_inc(done, 1)

            def products(dst, xs, ws, first, last):
                pe.matmul(dst, xs[0], ws[0], start=first, stop=False)
                pe.matmul(dst, xs[0], ws[1], start=False, stop=False)
                return pe.matmul(dst, xs[1], ws[0], start=False, stop=last)

            pe.wait_ge(s_const, 12)
            pe.wait_ge(s_rw, 32)
            with pe.Fori(0, B) as b:
                def quantised(j, off):
                    pe.wait_ge(s_quant, b * (2 * BT) + j + (off + 1))
                    pe.wait_ge(s_qlo, b * (4 * BT) + j * 2 + 2 * off)
                    for c in range(2):
                        transposes(bank[c], wide(1), c, s_qT)

                with pe.Fori(0, BT) as j:
                    quantised(j, 0)

                def first(j, off):
                    quantised(j * 2, BT + off)
                    pe.wait_ge(s_qlo, b * (4 * BT) + j * 4 + (2 * BT + 2 * off + 2))
                    pe.wait_ge(s_x1, b * BT + j * 2 + off)
                    for h in range(2):
                        cols = slice(512 * h, 512 * h + 512)
                        for k in range(KB):
                            last = products(bank[6 + h][:], (xT_hi[:, k, :], xT_lo[:, k, :]),
                                            (ctxT_hi[:, k, cols], ctxT_lo[:, k, cols]), k == 0, k == KB - 1)
                    last.then_inc(s_prod, 1)

                def second(j, off):
                    pe.wait_ge(s_norm, b * BT + j * 2 + (off + 1))
                    pe.wait_ge(s_nTs, b * (2 * BT) + j * 4 + 2 * off)
                    for c in range(2):
                        transposes(bank[2 + c], wide(3), c, s_nT)
                    pe.wait_ge(s_nTs, b * (2 * BT) + j * 4 + (2 * off + 2))
                    pe.wait_ge(s_logit_s, b * BT + j * 2 + off)
                    for k in range(KB):
                        last = pe.matmul(bank[4][:, 0:E], wide(5)[:, k * P:(k + 1) * P], rw[:, k, :], start=k == 0, stop=k == KB - 1)
                    last.then_inc(s_logit, 1)

                token_tiles(pe, first, second)

            pe.wait_ge(s_sel, 1)
            for n, m in ((0, tri), (2, ones)):
                for c in range(2):
                    pe.matmul(bank[n + c][:], m[:], sel_e[:, 512 * c:512 * c + 512], start=True, stop=True).then_inc(s_count, 1)

            def gathered(n, k, rows):
                pe.wait_ge(s_gath[n], rows)
                for c in range(2):
                    transposes(bank[c], row_in_t[n], c, s_xT)

            w_of = lambda c, n: tuple(w[:, c, :].rearrange("p (k n) -> p k n", n=n) for w in (w_hi, w_lo))
            pe.wait_ge(s_slots, 1)
            gathered(0, 0, 16)
            pe.wait_ge(s_meta, 16)
            with pe.Fori(0, NT // 2) as it:
                for n in range(2):
                    t = it * 2 + n
                    set_no = pe.value_load(tile_row[0:1, 0, bass.ds(t, 1)], min_val=0, max_val=NE - 1)
                    pe.wait_ge(s_xlo, t * 2 + 2)
                    pe.wait_ge(s_wlo, set_no * 3 + 1)
                    hi, lo = w_of(0, I)
                    for k in range(KB):
                        last = products(bank[2][:], (xT_hi[:, k, :], xT_lo[:, k, :]), (hi[:, k, :], lo[:, k, :]), k == 0, k == KB - 1)
                    last.then_inc(s_gate, 1)
                    pe.wait_ge(s_wlo, set_no * 3 + 2)
                    hi, lo = w_of(1, I)

                    def hidden(u):
                        pe.wait_ge(s_h, t * 2 + (u + 1))
                        pe.wait_ge(s_hlo, t * 2 + u)
                        for m in range(2):
                            last = pe.transpose(bank[5][:, m * P:(m + 1) * P], hid[:, (2 * u + m) * P:(2 * u + m + 1) * P], ident[:])
                        last.then_inc(s_hT, 1)

                    for u in range(2):
                        cols = slice(256 * u, 256 * u + 256)
                        for k in range(KB):
                            if u == 1 and k == KB // 2:
                                hidden(0)
                            last = products(bank[3 + u][:, 0:256], (xT_hi[:, k, :], xT_lo[:, k, :]),
                                            (hi[:, k, cols], lo[:, k, cols]), k == 0, k == KB - 1)
                        last.then_inc(s_up, 1)
                    gathered(1 - n, t + 1, it * 16 + (16 + 16 * n))
                    hidden(1)
                    pe.wait_ge(s_wlo, set_no * 3 + 3)
                    pe.wait_ge(s_y, t * 2)
                    hi, lo = w_of(2, H)
                    for u in range(2):
                        pe.wait_ge(s_hlo, t * 2 + (u + 1))
                        for h in range(2):
                            cols = slice(512 * h, 512 * h + 512)
                            for m in (2 * u, 2 * u + 1):
                                last = products(bank[6 + h][:], (hT_hi[:, m, :], hT_lo[:, m, :]),
                                                (hi[:, m, cols], lo[:, m, cols]), m == 0, m == IB - 1)
                            if u == 1:
                                last.then_inc(s_down, 1)


_INS = ['x', 'ctx_2048', 'L0_ffn_router_w', 'L0_ffn_router_bias', 'L0_ffn_w_gate', 'L0_ffn_w_up', 'L0_ffn_w_down',
        'L0_ffn_sw_gate', 'L0_ffn_sw_up', 'L0_ffn_sw_down']


def kernel(**inputs):
    import numpy as _np
    import concourse.bacc as _bacc
    from concourse import mybir as _mybir
    from concourse.bass_utils import run_bass_kernel_spmd as _run

    nc = _bacc.Bacc("TRN2", target_bir_lowering=False, num_devices=1)
    arrays, args = {}, []
    for name in _INS:
        a = _np.ascontiguousarray(inputs[name])
        arrays[f"in_{name}_dram"] = a
        args.append(nc.dram_tensor(f"in_{name}_dram", a.shape, _mybir.dt.from_np(a.dtype), kind="ExternalInput").ap())
    args.append(nc.dram_tensor("out_0_dram", (T + P, H), F32, kind="ExternalOutput").ap())
    xattn_moe_program(nc, *args)
    r = _run(nc, [arrays], core_ids=[0])
    return r.results[0]["out_0_dram"][:T].reshape(B, S, H)
```

```python
import concourse.bass as bass
from concourse import mybir
from contextlib import ExitStack

F32 = mybir.dt.float32
F32R = mybir.dt.float32r
BF16 = mybir.dt.bfloat16
I32 = mybir.dt.int32
U32 = mybir.dt.uint32
ALU = mybir.AluOpType
ACT = mybir.ActivationFunctionType
AX_X = mybir.AxisListType.X
RMAX = bass.bass_isa.ReduceOp.max

P = 128
B, S, H = 4, 1024, 1024
T = B * S
TT = T // P
BT = S // P
KB = H // P
E, G, TOPG, TOPK = 32, 8, 4, 8
EG = E // G
I = 512
IB = I // P
SH = 2
LN_EPS, ACT_EPS, W_EPS, FP8_MAX = 1e-5, 1e-4, 1e-6, 448.0
ROUTED_SCALE = 2.5
SHT = SH * TT
RT = (T * TOPK + (P - 1) * E) // P + 1
NT = SHT + RT
LT = NT + 3
NE = SH + E
CH = KB * I
PARTS = 4
CP = CH // PARTS
MT = 3 * P
MAGIC = 1.5 * 2.0 ** 23
LOG2E, LN2_HI, LN2_LO = 1.4426950408889634, 0.693145751953125, 1.42860677e-06
EXP_C = [1.0, 1 / 2, 1 / 6, 1 / 24, 1 / 120, 1 / 720, 1 / 5040]
TAKEN = -3.0e38
assert NT % 2 == 0 and NT <= MT - 1 and IB * H == CH


def xattn_moe_program(nc, x, ctx_in, router_w, router_b, w_gate, w_up, w_down, sw_gate, sw_up, sw_down, out):
    x_rows = x.rearrange("b s h -> (b s) h")
    ctx_rows = ctx_in.rearrange("b s h -> (b s) h")
    tokens = nc.dram_tensor("tokens", [T + P, H], F32, kind="Internal").ap()
    slots = nc.dram_tensor("slots", [P * LT, 2], I32, kind="Internal").ap()
    tile_sets = nc.dram_tensor("tile_sets", [2, MT], I32, kind="Internal").ap()

    with ExitStack() as stack:
        def sb(name, shape, dt=F32):
            return stack.enter_context(nc.sbuf_tensor(name, shape, dt))

        def sem(name):
            return stack.enter_context(nc.semaphore(name))

        w_hi = sb("w_hi", [P, 3, CH], F32R)
        w_lo = sb("w_lo", [P, 3, CH], F32R)
        w_raw = sb("w_raw", [P, 3, CH])
        xT_hi = sb("xT_hi", [P, KB, P], F32R)
        xT_lo = sb("xT_lo", [P, KB, P], F32R)
        hT_hi = sb("hT_hi", [P, IB, P], F32R)
        hT_lo = sb("hT_lo", [P, IB, P], F32R)
        row_in = sb("row_in", [P, 2, H])
        row_out = sb("row_out", [P, 2, H])
        row_in_t = [row_in[:, n, :] for n in range(2)]
        row_out_t = [row_out[:, n, :] for n in range(2)]
        scr = sb("scr", [P, 7, H])
        sel_e = sb("sel_e", [P, TT * E], BF16)
        ident = sb("ident", [P, P])
        tri = sb("tri", [P, P], BF16)
        ones = sb("ones", [P, P], BF16)
        rw = sb("rw", [P, KB, E])
        bias = sb("bias", [P, E])
        stats = [sb(f"stats{n}", [P, 2, 6]) for n in range(2)]
        mv = [sb(f"mv{n}", [P, 2]) for n in range(2)]
        sm = [sb(f"sm{n}", [P, 6]) for n in range(2)]
        sd = [sb(f"sd{n}", [P, 1]) for n in range(2)]
        amax = sb("amax", [P, KB])
        amax_c = sb("amax_c", [P, KB])
        amax_all = [sb(f"amax_all{n}", [P, KB]) for n in range(2)]
        qscale = [sb(f"qscale{n}", [P, 3, KB]) for n in range(2)]
        ef = sb("ef", [P, 8, E])
        ei = sb("ei", [P, E], I32)
        pick = sb("pick", [P, 2, E])
        top8 = sb("top8", [P, 8])
        token_no = sb("token_no", [P, TT], I32)
        tile_no = sb("tile_no", [P, 3], I32)
        tile_f = sb("tile_f", [P, 2, 3])
        tile_c = sb("tile_c", [P, 3, 3])
        set_i = sb("set_i", [P, 2, 3], I32)
        stage_rows = sb("stage_rows", [P, TOPK], I32)
        stage_picks = sb("stage_picks", [P, 2 * TOPK], I32)
        idx_g = [sb(f"idx_g{n}", [P, 2], I32) for n in range(2)]
        idx_s = [sb(f"idx_s{n}", [P, 2], I32) for n in range(2)]
        bank = [stack.enter_context(nc.psum_tensor(f"bank{n}", [P, 512], F32)) for n in range(8)]

        s_const = sem("s_const")
        s_init = sem("s_init")
        s_rw = sem("s_rw")
        s_cin = [sem("s_cin0"), sem("s_cin1")]
        s_xin = [sem("s_xin0"), sem("s_xin1")]
        s_var = [sem("s_var0"), sem("s_var1")]
        s_sqrt = [sem("s_sqrt0"), sem("s_sqrt1")]
        s_amax = sem("s_amax")
        s_amax_all = sem("s_amax_all")
        s_scaled = sem("s_scaled")
        s_round = sem("s_round")
        s_back = sem("s_back")
        s_zq = sem("s_zq")
        s_qT = sem("s_qT")
        s_qhi = sem("s_qhi")
        s_qlo = sem("s_qlo")
        s_prod = sem("s_prod")
        s_x1 = sem("s_x1")
        s_root = sem("s_root")
        s_x1_st = [sem("s_x1_st0"), sem("s_x1_st1")]
        s_norm = sem("s_norm")
        s_norm_st = sem("s_norm_st")
        s_nT = sem("s_nT")
        s_nTs = sem("s_nTs")
        s_logit = sem("s_logit")
        s_logit_s = sem("s_logit_s")
        s_dve = sem("s_dve")
        s_passed = sem("s_passed")
        s_dve_ctx = sem("s_dve_ctx")
        s_dve_q = sem("s_dve_q")
        s_dve_p = sem("s_dve_p")
        s_dve_r = sem("s_dve_r")
        s_sel = sem("s_sel")
        s_count = sem("s_count")
        s_slots = sem("s_slots")
        s_sets = sem("s_sets")
        s_meta_st = sem("s_meta_st")
        s_meta = sem("s_meta")
        s_stage = sem("s_stage")
        s_slot_st = sem("s_slot_st")
        s_raw = [sem(f"s_raw{c}") for c in range(3)]
        s_whi = sem("s_whi")
        s_wlo = sem("s_wlo")
        s_idx_g = [sem("s_idx_g0"), sem("s_idx_g1")]
        s_idx_s = [sem("s_idx_s0"), sem("s_idx_s1")]
        s_gath = [sem("s_gath0"), sem("s_gath1")]
        s_add = [sem("s_add0"), sem("s_add1")]
        s_xT = sem("s_xT")
        s_xhi = sem("s_xhi")
        s_xlo = sem("s_xlo")
        s_gate = sem("s_gate")
        s_up = sem("s_up")
        s_silu = sem("s_silu")
        s_h = sem("s_h")
        s_hT = sem("s_hT")
        s_hhi = sem("s_hhi")
        s_hlo = sem("s_hlo")
        s_down = sem("s_down")
        s_y = sem("s_y")

        block = stack.enter_context(nc.Block())
        v3 = lambda ap, a, b: ap.rearrange("p (a b) -> p a b", a=a, b=b)
        ctxT_hi = w_hi.rearrange("p c n -> p (c n)")[:, 0:KB * S].rearrange("p (k n) -> p k n", k=KB)
        ctxT_lo = w_lo.rearrange("p c n -> p (c n)")[:, 0:KB * S].rearrange("p (k n) -> p k n", k=KB)
        wide = lambda n: scr[:, n, :]
        NP = TT * TOPK
        slot_f = scr[:, 4, 0:NP].rearrange("p (i k) -> p i k", k=TOPK)
        slot_rows = scr[:, 4, NP:2 * NP].bitcast(I32)
        picks = scr[:, 4, 2 * NP:4 * NP].bitcast(I32).rearrange("p (n two) -> p n two", two=2)
        slot_i = scr[:, 0, 0:2 * NP].bitcast(I32).rearrange("p (a n) -> p a n", a=2)
        tile_row = scr[0:1, 1, 0:2 * MT].bitcast(I32).rearrange("o (d m) -> o d m", d=2)
        silu, hid = scr[:, 0, 0:I], scr[:, 0, I:2 * I]

        raw_rows = w_raw.rearrange("p c n -> p (c n)").rearrange("p (r n) -> p r n", n=H)
        quot = [raw_rows[:, n, :] for n in range(2)]
        step = raw_rows[:, 2, :]
        xhat = raw_rows[:, 3, :]
        xin = raw_rows[:, 4:8, :].rearrange("p r n -> p (r n)")
        cin = raw_rows[:, 8:12, :].rearrange("p r n -> p (r n)")

        def ring(buf, q, off):
            at = ((q * 2 + off) % 4) * H
            return buf[:, bass.ds(at, H)]

        class At:

            def __init__(self, b, q, off):
                self.bv, self.bo = b
                self.q, self.off = q, off
                self.n = off % 2

            def lag(self, n):
                return At((self.bv, self.bo), self.q, self.off - n)

            def real(self):
                return 0 <= self.off < BT

            def count(self, per, batch, more=0):
                return self.bv * batch + self.q * (2 * per) + (self.bo * batch + self.off * per + more)

            def half(self, per, batch, more=0):
                return self.bv * batch + self.q * per + (self.bo * batch + (self.off // 2) * per + more)

        def after(eng, s, n):
            if not isinstance(n, int) or n > 0:
                eng.wait_ge(s, n)

        def phase_a(eng, ctx_step, tok_step):
            def context(b, before):
                for j in range(4):
                    if before is not None:
                        tok_step(At(before, 0, BT + j))
                    ctx_step(At(b, 0, j))
                with eng.Fori(0, 2) as q:
                    ctx_step(At(b, q, 4))
                    ctx_step(At(b, q, 5))

            def tokens_of(b):
                for j in range(4):
                    if j < 2:
                        ctx_step(At(b, 0, BT + j))
                    tok_step(At(b, 0, j))
                with eng.Fori(0, 2) as q:
                    tok_step(At(b, q, 4))
                    tok_step(At(b, q, 5))

            context((0, 0), None)
            with eng.Fori(0, B - 1) as b:
                tokens_of((b, 0))
                context((b, 1), (b, 0))
            tokens_of((0, B - 1))
            for j in range(4):
                tok_step(At((0, B - 1), 0, BT + j))

        @block.sync
        def _(sp):
            sp.dma_start(rw[:], router_w.rearrange("(k p) e -> p k e", p=P)).then_inc(s_rw, 16)
            sp.dma_start(bias[:], router_b.partition_broadcast(P)).then_inc(s_rw, 16)
            def ctx_load(t):
                if t.real():
                    after(sp, s_scaled, t.count(1, 2 * BT, -3) if t.off >= 4 else t.count(1, 2 * BT, -BT - 3))
                    sp.sem_inc(s_passed)
                    after(sp, s_cin[t.n], t.half(16, 8 * BT))
                    sp.sem_inc(s_passed)
                    sp.dma_start(ring(cin, t.q, t.off), ctx_rows[bass.ds(t.count(P, S), P), :]).then_inc(s_cin[t.n], 16)

            def tok_load(t):
                if t.real():
                    after(sp, s_x1, t.count(1, BT, -min(t.off, 3)))
                    sp.sem_inc(s_passed)
                    after(sp, s_xin[t.n], t.half(16, 8 * BT))
                    sp.sem_inc(s_passed)
                    sp.dma_start(ring(xin, t.q, t.off), x_rows[bass.ds(t.count(P, S), P), :]).then_inc(s_xin[t.n], 16)

            phase_a(sp, ctx_load, tok_load)
            sp.wait_ge(s_x1, TT)

            def chunk(c, s):
                return w_raw[:, c, :].rearrange("p (k n) -> p k n", n=s)

            for s in range(SH):
                for c, src in enumerate((sw_gate, sw_up, sw_down)):
                    if s > 0:
                        sp.wait_ge(s_wlo, PARTS * (3 * (s - 1) + c + 1))
                    if c < 2:
                        sp.dma_start(chunk(c, I), src[:, s * I:(s + 1) * I].rearrange("(k p) n -> p k n", p=P)).then_inc(s_raw[c], 16)
                    else:
                        sp.dma_start(chunk(c, H), src[s * I:(s + 1) * I, :].rearrange("(k p) n -> p k n", p=P)).then_inc(s_raw[c], 16)
            with sp.Fori(0, E) as e:
                for c, src in enumerate((w_gate, w_up, w_down)):
                    sp.wait_ge(s_wlo, e * (3 * PARTS) + PARTS * (3 * (SH - 1) + c + 1))
                    rows = src.rearrange("e k n -> (e k) n")[bass.ds(e * src.shape[1], src.shape[1]), :]
                    sp.dma_start(chunk(c, src.shape[2]), rows.rearrange("(k p) n -> p k n", p=P)).then_inc(s_raw[c], 16)

        @block.gpsimd
        def _(pool):
            pool.memset(ident[:], 0.0).then_inc(s_const, 1)
            pool.memset(tri[:], 1.0).then_inc(s_const, 1)
            pool.memset(ones[:], 1.0).then_inc(s_const, 1)
            pool.memset(wide(6), 0.0).then_inc(s_const, 1)
            table = scr[:, 4, 0:2 * LT].bitcast(I32).rearrange("p (t two) -> p t two", two=2)
            weight = scr[:, 4, 0:2 * LT].rearrange("p (t two) -> p t two", two=2)
            pool.iota(table[:, 0:SHT, 0:1], [[0, SH], [P, TT], [0, 1]], base=0, channel_multiplier=1).then_inc(s_const, 1)
            pool.iota(table[:, SHT:LT, 0:1], [[0, LT - SHT], [0, 1]], base=T, channel_multiplier=1).then_inc(s_const, 1)
            pool.memset(weight[:, 0:SHT, 1:2], 1.0).then_inc(s_const, 1)
            pool.memset(weight[:, SHT:LT, 1:2], 0.0).then_inc(s_const, 1)
            pool.iota(token_no[:], [[P, TT]], base=0, channel_multiplier=1).then_inc(s_const, 1)
            pool.iota(tile_no[:], [[P, 3]], base=0, channel_multiplier=1).then_inc(s_const, 1)
            pool.wait_ge(s_const, 10)
            pool.affine_select(out=ident[:], in_=ident[:], compare_op=ALU.not_equal, fill=1.0,
                               base=0, pattern=[[-1, P]], channel_multiplier=1).then_inc(s_const, 1)
            pool.affine_select(out=tri[:], in_=tri[:], compare_op=ALU.is_gt, fill=0.0,
                               base=0, pattern=[[1, P]], channel_multiplier=-1).then_inc(s_const, 1)
            pool.dma_start(slots.rearrange("(p t) two -> p (t two)", p=P), scr[:, 4, 0:2 * LT].bitcast(I32)).then_inc(s_init, 16)
            pool.dma_start(tokens[T:T + P, :], wide(6)).then_inc(s_init, 16)
            pool.dma_start(out[T:T + P, :], wide(6)).then_inc(s_init, 16)
            pool.wait_ge(s_init, 48)

            def round_job(g, n):
                pool.wait_ge(s_scaled, g + 1)
                pool.tensor_tensor(quot[n], quot[n], step, ALU.add).then_inc(s_zq, 1)
                pool.wait_ge(s_zq, g + 1)
                pool.tensor_tensor(quot[n], quot[n], step, ALU.subtract).then_inc(s_round, 1)

            def ctx_step(t):
                if t.real():
                    pool.wait_ge(s_amax, t.count(1, BT, 1))
                    after(pool, s_scaled, t.count(1, 2 * BT, -1) if t.off >= 2 else t.count(1, 2 * BT, -BT - 1))
                    pool.sem_inc(s_passed)
                    pool.partition_all_reduce(amax_all[t.n][:], amax_c[:], P, RMAX).then_inc(s_amax_all, 1)
                t = t.lag(1)
                if t.real():
                    round_job(t.count(1, 2 * BT), t.n)

            def tok_step(t):
                z = t.lag(3)
                if z.real():
                    pool.wait_ge(s_norm, z.count(1, BT, 1))
                    pool.sem_inc(s_passed)
                    pool.dma_start(tokens[bass.ds(z.count(P, S), P), :], wide(3)).then_inc(s_norm_st, 16)
                if t.real():
                    round_job(t.count(1, 2 * BT, BT), t.n)
                z = t.lag(2)
                if z.real():
                    pool.wait_ge(s_x1, z.count(1, BT, 1))
                    pool.sem_inc(s_passed)
                    pool.dma_start(out[bass.ds(z.count(P, S), P), :], row_out_t[z.n]).then_inc(s_x1_st[z.n], 16)

            phase_a(pool, ctx_step, tok_step)
            for n in range(2):
                pool.wait_ge(s_x1_st[n], 16 * (TT // 2))
            pool.wait_ge(s_norm_st, 16 * TT)

            slot_tiles = slots.rearrange("(p t) two -> p t two", p=P)

            def load_idx(dst, t, done):
                pool.dma_start(dst[:], slot_tiles[:, bass.ds(t, 1), :].rearrange("p t two -> p (t two)")).then_inc(done, 16)

            def gather(n):
                pool.indirect_dma_start(out=row_in_t[n], out_offset=None, in_=tokens[:, :],
                                        in_offset=bass.IndirectOffsetOnAxis(ap=idx_g[n][:, 0:1].bitcast(U32), axis=0)).then_inc(s_gath[n], 16)

            def tile_step(it, n):
                pool.wait_ge(s_idx_g[n], it * 16 + 32)
                pool.wait_ge(s_xT, it * 4 + (2 * n + 2))
                pool.sem_inc(s_passed)
                gather(n)
                pool.wait_ge(s_gath[1 - n], it * 16 + (16 + 16 * n))
                pool.sem_inc(s_passed)
                if n == 0:
                    load_idx(idx_g[1], it * 2 + 3, s_idx_g[1])
                else:
                    load_idx(idx_g[0], it * 2 + 4, s_idx_g[0])
                pool.wait_ge(s_y, it * 4 + (2 * n + 2))
                if n == 0:
                    pool.wait_ge(s_add[1], it * 16)
                else:
                    pool.wait_ge(s_add[0], it * 16 + 16)
                pool.sem_inc(s_passed)
                pool.indirect_dma_start(out=out[:, :], out_offset=bass.IndirectOffsetOnAxis(ap=idx_s[n][:, 0:1].bitcast(U32), axis=0),
                                        in_=row_out_t[n], in_offset=None, compute_op=ALU.add).then_inc(s_add[n], 16)
                pool.wait_ge(s_add[n], it * 16 + 16)
                pool.sem_inc(s_passed)
                load_idx(idx_s[n], it * 2 + (n + 2), s_idx_s[n])

            for n in range(2):
                load_idx(idx_g[n], n, s_idx_g[n])
                load_idx(idx_s[n], n, s_idx_s[n])
            for n in range(2):
                pool.wait_ge(s_idx_g[n], 16)
                gather(n)
            pool.wait_ge(s_gath[0], 16)
            load_idx(idx_g[0], 2, s_idx_g[0])

            pool.wait_ge(s_sets, 1)
            for d in range(2):
                with nc.allow_non_contiguous_dma(reason="three values per partition"):
                    pool.dma_start(tile_sets[d:d + 1, :].rearrange("a (c p) -> p (a c)", p=P), set_i[:, d, :]).then_inc(s_meta_st, 16)
            pool.wait_ge(s_meta_st, 32)
            pool.dma_start(tile_row, tile_sets[:, :].rearrange("(o d) m -> o d m", o=1)).then_inc(s_meta, 16)

            pool.wait_ge(s_slots, 1)
            pool.wait_ge(s_init, 48)
            last_shared = SHT // 2 - 2
            with pool.Fori(0, TT) as i:
                pool.wait_ge(s_slot_st, i * (16 * TOPK))
                pool.tensor_copy(stage_rows[:], slot_rows[:, bass.ds(i * TOPK, TOPK)]).then_inc(s_stage, 1)
                pool.tensor_copy(stage_picks[:], picks.rearrange("p n two -> p (n two)")[:, bass.ds(i * (2 * TOPK), 2 * TOPK)]).then_inc(s_stage, 1)
                pool.wait_ge(s_stage, i * 2 + 2)
                pool.sem_inc(s_passed)
                for k in range(TOPK):
                    pool.indirect_dma_start(out=slots[:, :], out_offset=bass.IndirectOffsetOnAxis(ap=stage_rows[:, k:k + 1].bitcast(U32), axis=0),
                                            in_=stage_picks[:, 2 * k:2 * k + 2], in_offset=None).then_inc(s_slot_st, 16)
                with pool.If(i < last_shared):
                    for n in range(2):
                        tile_step(i, n)
            pool.wait_ge(s_slot_st, 16 * TOPK * TT)
            with pool.Fori(last_shared, NT // 2) as it:
                for n in range(2):
                    tile_step(it, n)
            for n in range(2):
                pool.wait_ge(s_add[n], 16 * (NT // 2))
                pool.wait_ge(s_idx_g[n], 16 * (NT // 2 + 1) + (16 if n == 0 else 0))
                pool.wait_ge(s_idx_s[n], 16 * (NT // 2 + 1))
                pool.wait_ge(s_gath[n], 16 * (NT // 2 + 1))

        @block.scalar
        def _(act):
            def root(k, t):
                act.wait_ge(s_var[k], t.count(1, BT, 1))
                act.activation(sd[k][:], sm[k][:, 0:1], ACT.Sqrt).then_inc(s_sqrt[k], 1)

            def ctx_step(t):
                t = t.lag(2)
                if t.real():
                    after(act, s_prod, t.bv * BT + t.bo * BT)
                    for k in range(KB):
                        if k % 4 == 0:
                            act.wait_ge(s_qT, t.count(2, 4 * BT, k // 4 + 1))
                        ins = act.activation(ctxT_hi[:, k, bass.ds(t.q * (2 * P) + t.off * P, P)], bank[k // 4][:, (k % 4) * P:(k % 4 + 1) * P],
                                             ACT.Copy, scale=qscale[t.n][:, 2, k:k + 1])
                        if k % 4 == 3:
                            ins.then_inc(s_qhi, 1)

            def tok_step(t):
                if t.real():
                    root(0, t)
                z = t.lag(3)
                if z.real():
                    act.wait_ge(s_root, z.count(1, BT, 1))
                    after(act, s_norm_st, z.count(16, 16 * BT))
                    after(act, s_nT, z.count(2, 2 * BT))
                    act.activation(wide(3), row_out_t[z.n], ACT.Identity, bias=sm[1][:, 5:6], scale=sm[1][:, 4:5]).then_inc(s_norm, 1)
                z = t.lag(1)
                if z.real():
                    after(act, s_prod, z.count(1, BT))
                    for c in range(2):
                        act.wait_ge(s_qT, z.count(2, 4 * BT, 2 * BT + c + 1))
                        act.activation(xT_hi[:, 4 * c:4 * c + 4, :], v3(bank[c][:], 4, P), ACT.Copy).then_inc(s_qhi, 1)
                z = t.lag(4)
                if z.real():
                    act.wait_ge(s_logit, z.count(1, BT, 1))
                    act.activation(wide(6)[:, bass.ds(z.count(E, BT * E), E)], bank[4][:, 0:E], ACT.Copy).then_inc(s_logit_s, 1)
                z = t.lag(3)
                if z.real():
                    after(act, s_logit, z.count(1, BT))
                    for c in range(2):
                        act.wait_ge(s_nT, z.count(2, 2 * BT, c + 1))
                        act.activation(wide(5)[:, c * 512:(c + 1) * 512], bank[2 + c][:], ACT.Copy).then_inc(s_nTs, 1)
                z = t.lag(2)
                if z.real():
                    root(1, z)
                if t.real():
                    act.wait_ge(s_round, t.count(1, 2 * BT, BT + 1))
                    for k in range(KB):
                        ins = act.activation(quot[t.n][:, k * P:(k + 1) * P], quot[t.n][:, k * P:(k + 1) * P], ACT.Copy, scale=qscale[t.n][:, 2, k:k + 1])
                    ins.then_inc(s_back, 1)

            phase_a(act, ctx_step, tok_step)

            def split_hi(c, loaded):
                act.wait_ge(s_raw[c], loaded)
                for s in range(PARTS):
                    part = slice(s * CP, (s + 1) * CP)
                    act.activation(w_hi[:, c, part], w_raw[:, c, part], ACT.Copy).then_inc(s_whi, 1)

            def gathered_hi(k):
                for c in range(2):
                    act.wait_ge(s_xT, k * 2 + (c + 1))
                    act.activation(xT_hi[:, 4 * c:4 * c + 4, :], v3(bank[c][:], 4, P), ACT.Copy).then_inc(s_xhi, 1)

            act.wait_ge(s_prod, TT)
            for c in range(3):
                split_hi(c, 16)
            gathered_hi(0)
            act.wait_ge(s_meta, 16)
            with act.Fori(0, NT // 2) as it:
                for n in range(2):
                    t = it * 2 + n
                    last = act.value_load(tile_row[0:1, 1, bass.ds(t, 1)], min_val=0, max_val=1)
                    set_no = act.value_load(tile_row[0:1, 0, bass.ds(t, 1)], min_val=0, max_val=NE - 1)
                    act.wait_ge(s_gate, t + 1)
                    act.wait_ge(s_h, t * 2)
                    act.activation(silu[:], bank[2][:], ACT.Silu).then_inc(s_silu, 1)
                    with act.If(last > 0):
                        split_hi(0, set_no * 16 + 32)
                    for u in range(2):
                        act.wait_ge(s_hT, t * 2 + (u + 1))
                        act.activation(hT_hi[:, 2 * u:2 * u + 2, :], v3(bank[5][:, 0:256], 2, P), ACT.Copy).then_inc(s_hhi, 1)
                    act.wait_ge(s_up, t * 2 + 2)
                    gathered_hi(t + 1)
                    with act.If(last > 0):
                        split_hi(1, set_no * 16 + 32)
                        act.wait_ge(s_down, t * 2 + 2)
                        split_hi(2, set_no * 16 + 32)
                    for c in range(2):
                        act.wait_ge(s_down, t * 2 + (c + 1))
                        if c == 0:
                            act.wait_ge(s_idx_s[n], it * 16 + 16)
                            if n == 0:
                                act.wait_ge(s_add[0], it * 16)
                            else:
                                act.wait_ge(s_add[1], it * 16)
                        act.activation(row_out_t[n][:, c * 512:(c + 1) * 512], bank[6 + c][:], ACT.Copy,
                                       scale=idx_s[n][:, 1:2].bitcast(F32)).then_inc(s_y, 1)

        @block.vector
        def _(v):
            chain = [None, 0, 0]

            def start(s, before):
                chain[:] = [s, before, 0]

            def link(ins):
                chain[2] += 1
                ins.then_inc(chain[0], 1)
                v.wait_ge(chain[0], chain[1] + chain[2])

            def moments(src, k):
                v.bn_stats(stats[k][:, 0, :], src[:, 0:512])
                link(v.bn_stats(stats[k][:, 1, :], src[:, 512:1024]))
                v.sem_inc(s_passed)
                link(v.bn_aggr(mv[k][:], stats[k].rearrange("p a b -> p (a b)")))
                v.tensor_scalar(sm[k][:, 0:1], mv[k][:, 1:2], LN_EPS, None, ALU.add).then_inc(s_var[k], 1)

            def inverse_root(k):
                m = sm[k]
                link(v.reciprocal(m[:, 1:2], sd[k][:]))
                link(v.scalar_tensor_tensor(m[:, 2:3], m[:, 1:2], m[:, 0:1], m[:, 1:2], ALU.mult, ALU.mult))
                link(v.tensor_scalar(m[:, 3:4], m[:, 2:3], -0.5, 1.5, ALU.mult, ALU.add))
                link(v.tensor_tensor(m[:, 4:5], m[:, 3:4], m[:, 1:2], ALU.mult))

            def scale(src, maxima, eps, n, g):
                qs = qscale[n]
                link(v.tensor_scalar(qs[:, 0, :], maxima, eps, None, ALU.max))
                link(v.reciprocal(qs[:, 1, :], qs[:, 0, :]))
                v.tensor_scalar(qs[:, 1, :], qs[:, 1, :], FP8_MAX, None, ALU.mult)
                link(v.tensor_scalar(qs[:, 2, :], qs[:, 0, :], 1.0 / FP8_MAX, None, ALU.mult))
                link(v.tensor_tensor(v3(quot[n], KB, P), v3(src, KB, P), qs[:, 1, :].unsqueeze(2).to_broadcast([P, KB, P]), ALU.mult))
                after(v, s_round, g)
                link(v.tensor_scalar(step.bitcast(U32), quot[n].bitcast(U32), 0x7F800000, None, ALU.bitwise_and))
                v.tensor_scalar(step, step, 2.0 ** -6, 1.5 * 2.0 ** 20, ALU.max, ALU.mult).then_inc(s_scaled, 1)

            K_CTX, K_Q, K_P, K_R = 5, 13, 2, 4

            def ctx_step(t):
                if t.real():
                    v.wait_ge(s_cin[t.n], t.half(16, 8 * BT, 16))
                    after(v, s_amax_all, t.count(1, BT))
                    v.tensor_reduce(amax_c[:], v3(ring(cin, t.q, t.off), KB, P), AX_X, ALU.max, apply_absolute_value=True).then_inc(s_amax, 1)
                z = t.lag(1)
                if z.real():
                    g = z.count(1, 2 * BT)
                    start(s_dve_ctx, z.count(K_CTX, BT * K_CTX))
                    v.wait_ge(s_amax_all, z.count(1, BT, 1))
                    after(v, s_qT, z.count(2, 4 * BT, -2))
                    scale(ring(cin, z.q, z.off), amax_all[z.n][:], W_EPS, z.n, g)
                    assert chain[2] == K_CTX, chain
                z = t.lag(2)
                if z.real():
                    at = bass.ds(z.q * (2 * P) + z.off * P, P)
                    for k in range(KB):
                        if k % 4 == 0:
                            v.wait_ge(s_qhi, z.count(2, 4 * BT, k // 4 + 1))
                        ins = v.scalar_tensor_tensor(ctxT_lo[:, k, at], bank[k // 4][:, (k % 4) * P:(k % 4 + 1) * P], qscale[z.n][:, 2, k:k + 1],
                                                     ctxT_hi[:, k, at].bitcast(F32), ALU.mult, ALU.subtract)
                        if k % 4 == 3:
                            ins.then_inc(s_qlo, 1)

            def tok_step(t):
                if t.real():
                    start(s_dve_q, t.count(K_Q, BT * K_Q))
                    v.wait_ge(s_xin[t.n], t.half(16, 8 * BT, 16))
                    moments(ring(xin, t.q, t.off), 0)
                    mine = list(chain)
                z = t.lag(3)
                if z.real():
                    start(s_dve_r, z.count(K_R, BT * K_R))
                    v.wait_ge(s_sqrt[1], z.count(1, BT, 1))
                    after(v, s_norm, z.count(1, BT))
                    inverse_root(1)
                    v.scalar_tensor_tensor(sm[1][:, 5:6], mv[1][:, 0:1], -1.0, sm[1][:, 4:5], ALU.mult, ALU.mult).then_inc(s_root, 1)
                    assert chain[2] == K_R, chain
                if t.real():
                    chain[:] = mine
                    v.wait_ge(s_sqrt[0], t.count(1, BT, 1))
                    inverse_root(0)
                    link(v.tensor_scalar(xhat, ring(xin, t.q, t.off), mv[0][:, 0:1], sm[0][:, 4:5], ALU.subtract, ALU.mult))
                    link(v.tensor_reduce(amax[:], v3(xhat, KB, P), AX_X, ALU.max, apply_absolute_value=True))
                    v.wait_ge(s_qT, t.count(2, 4 * BT, 2 * BT - 2))
                    scale(xhat, amax[:], ACT_EPS, t.n, t.count(1, 2 * BT, BT))
                    assert chain[2] == K_Q, chain
                z = t.lag(2)
                if z.real():
                    v.wait_ge(s_prod, z.count(1, BT, 1))
                    after(v, s_x1_st[z.n], z.half(16, 8 * BT))
                    after(v, s_norm, z.count(1, BT, -min(z.off, 1)))
                    for c in range(2):
                        cols = slice(c * 512, (c + 1) * 512)
                        ins = v.tensor_tensor(row_out_t[z.n][:, cols], bank[6 + c][:], ring(xin, z.q, z.off)[:, cols], ALU.add)
                    ins.then_inc(s_x1, 1)
                y = t.lag(1)
                if y.real():
                    for c in range(2):
                        v.wait_ge(s_qhi, y.count(2, 4 * BT, 2 * BT + c + 1))
                        v.tensor_tensor(xT_lo[:, 4 * c:4 * c + 4, :], v3(bank[c][:], 4, P),
                                        xT_hi[:, 4 * c:4 * c + 4, :].bitcast(F32), ALU.subtract).then_inc(s_qlo, 1)
                if z.real():
                    start(s_dve_p, z.count(K_P, BT * K_P))
                    v.wait_ge(s_x1, z.count(1, BT, 1))
                    after(v, s_root, z.count(1, BT))
                    moments(row_out_t[z.n], 1)
                    assert chain[2] == K_P, chain

            v.wait_ge(s_const, 12)
            phase_a(v, ctx_step, tok_step)

            def split_lo(c, parts, before):
                for s in parts:
                    part = slice(s * CP, (s + 1) * CP)
                    v.wait_ge(s_whi, before + (c * PARTS + s + 1))
                    v.tensor_tensor(w_lo[:, c, part], w_raw[:, c, part], w_hi[:, c, part].bitcast(F32), ALU.subtract).then_inc(s_wlo, 1)

            for c in range(3):
                split_lo(c, range(PARTS), 0)

            start(s_dve, 0)
            v.wait_ge(s_logit_s, TT)
            v.wait_ge(s_norm_st, 16 * TT)
            v.wait_ge(s_rw, 32)
            tte = lambda n: wide(n).rearrange("p (i e) -> p i e", e=E)
            link(v.tensor_scalar(wide(0), wide(6), -80.0, 80.0, ALU.max, ALU.min))
            link(v.tensor_scalar(wide(1), wide(0), -LOG2E, MAGIC, ALU.mult, ALU.add))
            link(v.tensor_scalar(wide(1), wide(1), MAGIC, None, ALU.subtract))
            link(v.scalar_tensor_tensor(wide(2), wide(1), -LN2_HI, wide(0), ALU.mult, ALU.subtract))
            link(v.scalar_tensor_tensor(wide(2), wide(1), -LN2_LO, wide(2), ALU.mult, ALU.add))
            link(v.tensor_scalar(wide(3), wide(2), EXP_C[-1], None, ALU.mult))
            for coef in EXP_C[-2::-1]:
                link(v.scalar_tensor_tensor(wide(3), wide(3), coef, wide(2), ALU.add, ALU.mult))
            link(v.tensor_scalar(wide(4).bitcast(I32), wide(1), 127.0, 2.0 ** 23, ALU.add, ALU.mult))
            link(v.scalar_tensor_tensor(wide(3), wide(3), 1.0, wide(4), ALU.add, ALU.mult))
            link(v.tensor_scalar(wide(3), wide(3), 1.0, None, ALU.add))
            link(v.reciprocal(wide(0), wide(3)))
            link(v.tensor_tensor(tte(1), tte(0), bias[:].unsqueeze(1).to_broadcast([P, TT, E]), ALU.add))
            four = wide(1).rearrange("p (q m) -> p q m", m=EG)
            col = lambda m: four[:, :, m]
            q4 = lambda n, m: wide(n)[:, 256 * m:256 * m + 256]
            v.tensor_tensor(q4(2, 0), col(0), col(1), ALU.max)
            v.tensor_tensor(q4(2, 1), col(0), col(1), ALU.min)
            v.tensor_tensor(q4(2, 2), col(2), col(3), ALU.max)
            link(v.tensor_tensor(q4(2, 3), col(2), col(3), ALU.min))
            v.tensor_tensor(q4(3, 0), q4(2, 0), q4(2, 2), ALU.max)
            v.tensor_tensor(q4(3, 1), q4(2, 0), q4(2, 2), ALU.min)
            link(v.tensor_tensor(q4(3, 2), q4(2, 1), q4(2, 3), ALU.max))
            link(v.tensor_tensor(q4(3, 1), q4(3, 1), q4(3, 2), ALU.max))
            link(v.tensor_tensor(q4(3, 3), q4(3, 0), q4(3, 1), ALU.add))
            gs = q4(3, 3).rearrange("p (i g) -> p i g", g=G)
            pairs = scr[:, 4:6, :].rearrange("p a (i g o) -> p (a i) g o", g=G, o=G)
            link(v.memset(scr[:, 4:6, :], 0.0))
            for o in range(G):
                if o > 0:
                    last = v.tensor_tensor(pairs[:, :, 0:o, o], gs[:, :, o].unsqueeze(2).to_broadcast([P, TT, o]), gs[:, :, 0:o], ALU.is_gt)
                if o < G - 1:
                    last = v.tensor_tensor(pairs[:, :, o + 1:G, o], gs[:, :, o].unsqueeze(2).to_broadcast([P, TT, G - 1 - o]), gs[:, :, o + 1:G], ALU.is_ge)
            link(last)
            link(v.tensor_reduce(q4(2, 0), pairs, AX_X, ALU.add))
            link(v.tensor_scalar(q4(2, 1), q4(2, 0), TOPG - 0.5, None, ALU.is_lt))
            keep = q4(2, 1).unsqueeze(2).to_broadcast([P, TT * G, EG])
            link(v.tensor_tensor(wide(3).rearrange("p (q m) -> p q m", m=EG), four, keep, ALU.mult))
            link(v.tensor_scalar(wide(3), wide(3), 0.0, None, ALU.add))
            before = chain[2]
            with v.Fori(0, TT) as i:
                start(s_dve, i * 4 + before)
                at = bass.ds(i * E, E)
                link(v.tensor_copy(pick[:, 0, :], wide(3)[:, at]))
                v.sem_inc(s_passed)
                link(v.max(top8[:], pick[:, 0, :]))
                v.sem_inc(s_passed)
                link(v.match_replace(pick[:, 1, :], top8[:], pick[:, 0, :], TAKEN))
                link(v.tensor_scalar(wide(4)[:, at], pick[:, 1, :], TAKEN, None, ALU.is_equal))
            start(s_dve, before + 4 * TT)
            v.tensor_copy(sel_e.rearrange("p (e i) -> p e i", i=TT), tte(4).rearrange("p i e -> p e i")).then_inc(s_sel, 1)
            link(v.tensor_tensor(wide(1), wide(0), wide(4), ALU.mult))
            link(v.tensor_reduce(ef[:, 0, :], tte(1), AX_X, ALU.add))
            link(v.reciprocal(ef[:, 1, :], ef[:, 0, :]))
            link(v.tensor_tensor(tte(1), tte(1), ef[:, 1, :].unsqueeze(2).to_broadcast([P, TT, E]), ALU.mult))
            link(v.tensor_scalar(wide(1), wide(1), ROUTED_SCALE, None, ALU.mult))
            link(v.memset(wide(3), 1.0))
            link(v.memset(tte(3)[:, :, 0:1], 0.0))
            v.wait_ge(s_count, 4)
            for c in range(2):
                last = v.tensor_copy(wide(2)[:, 512 * c:512 * c + 512], bank[2 + c][:])
            link(last)
            link(v.tensor_tensor_scan(wide(5), wide(3), wide(2), 0.0, ALU.mult, ALU.add))
            eti = lambda n: wide(n).rearrange("p (e i) -> p e i", i=TT)
            link(v.tensor_scalar(ei[:], eti(5)[:, :, TT - 1], float(P - 1), None, ALU.add))
            link(v.tensor_scalar(ei[:], ei[:], 7, None, ALU.logical_shift_right))
            link(v.tensor_scalar(ef[:, 2, :], ei[:], 1.0, None, ALU.max))
            link(v.memset(ef[:, 3, :], 1.0))
            link(v.tensor_tensor_scan(ef[:, 4, :], ef[:, 3, :], ef[:, 2, :], 0.0, ALU.mult, ALU.add))
            link(v.tensor_tensor(ef[:, 5, :], ef[:, 4, :], ef[:, 2, :], ALU.subtract))
            link(v.tensor_scalar(ef[:, 6, :], ef[:, 5, :], float(SHT), float(P), ALU.add, ALU.mult))
            link(v.tensor_scalar(ef[:, 7, :], ef[:, 4, :], float(SHT), None, ALU.add))
            link(v.tensor_tensor(wide(6), wide(5), wide(2), ALU.subtract))
            for c in range(2):
                last = v.tensor_tensor(wide(6)[:, 512 * c:512 * c + 512], bank[c][:], wide(6)[:, 512 * c:512 * c + 512], ALU.add)
            link(last)
            link(v.tensor_tensor(eti(6), eti(6), ef[:, 6, :].unsqueeze(2).to_broadcast([P, E, TT]), ALU.add))
            link(v.tensor_tensor_scan(wide(2), wide(3), wide(4), 0.0, ALU.mult, ALU.add))
            link(v.tensor_tensor(wide(2), wide(2), wide(4), ALU.mult))
            place = eti(6).rearrange("p e i -> p i e")
            picks_w = picks.bitcast(F32).rearrange("p (i k) two -> p i k two", k=TOPK)
            for k in range(TOPK):
                v.scalar_tensor_tensor(tte(3), tte(2), float(k + 1), place, ALU.is_equal, ALU.mult)
                link(v.scalar_tensor_tensor(tte(5), tte(2), float(k + 1), tte(1), ALU.is_equal, ALU.mult))
                v.tensor_reduce(slot_f[:, :, k], tte(3), AX_X, ALU.add)
                link(v.tensor_reduce(picks_w[:, :, k, 1], tte(5), AX_X, ALU.add))
            tok = token_no[:].unsqueeze(2).to_broadcast([P, TT, TOPK])
            v.tensor_copy(picks.rearrange("p (i k) two -> p i k two", k=TOPK)[:, :, :, 0], tok)
            link(v.tensor_copy(slot_i[:, 0, :], slot_f.rearrange("p i k -> p (i k)")))
            link(v.tensor_scalar(slot_i[:, 1, :], slot_i[:, 0, :], 7, None, ALU.logical_shift_right))
            link(v.tensor_scalar(slot_i[:, 0, :], slot_i[:, 0, :], P - 1, None, ALU.bitwise_and))
            v.scalar_tensor_tensor(slot_rows[:], slot_i[:, 0, :], float(LT), slot_i[:, 1, :], ALU.mult, ALU.add).then_inc(s_slots, 1)
            v.tensor_copy(tile_f[:, 0, :], tile_no[:])
            link(v.tensor_scalar(tile_f[:, 1, :], tile_no[:], 1.0, None, ALU.add))
            cmp = lambda d: wide(2 + d)[:, 0:3 * E].rearrange("p (c e) -> p c e", e=E)
            ends = ef[:, 7, :].unsqueeze(1).to_broadcast([P, 3, E])
            for d in range(2):
                link(v.tensor_tensor(cmp(d), tile_f[:, d, :].unsqueeze(2).to_broadcast([P, 3, E]), ends, ALU.is_ge))
                link(v.tensor_reduce(tile_c[:, d, :], cmp(d), AX_X, ALU.add))
                link(v.scalar_tensor_tensor(tile_c[:, d, :], tile_f[:, d, :], float(TT), tile_c[:, d, :], ALU.is_ge, ALU.add))
                link(v.scalar_tensor_tensor(tile_c[:, d, :], tile_f[:, d, :], float(SHT), tile_c[:, d, :], ALU.is_ge, ALU.add))
                link(v.tensor_scalar(tile_c[:, d, :], tile_c[:, d, :], float(NE - 1), None, ALU.min))
            v.tensor_copy(set_i[:, 0, :], tile_c[:, 0, :])
            v.tensor_tensor(set_i[:, 1, :], tile_c[:, 1, :], tile_c[:, 0, :], ALU.subtract).then_inc(s_sets, 1)

            def gathered_lo(k):
                for c in range(2):
                    v.wait_ge(s_xhi, k * 2 + (c + 1))
                    v.tensor_tensor(xT_lo[:, 4 * c:4 * c + 4, :], v3(bank[c][:], 4, P),
                                    xT_hi[:, 4 * c:4 * c + 4, :].bitcast(F32), ALU.subtract).then_inc(s_xlo, 1)

            gathered_lo(0)
            v.wait_ge(s_meta, 16)
            with v.Fori(0, NT // 2) as it:
                for n in range(2):
                    t = it * 2 + n
                    last = v.value_load(tile_row[0:1, 1, bass.ds(t, 1)], min_val=0, max_val=1)
                    set_no = v.value_load(tile_row[0:1, 0, bass.ds(t, 1)], min_val=0, max_val=NE - 1)
                    with v.If(last > 0):
                        split_lo(0, range(0, PARTS // 2), set_no * (3 * PARTS) + 3 * PARTS)
                    v.wait_ge(s_silu, t + 1)
                    for u in range(2):
                        cols = slice(256 * u, 256 * u + 256)
                        v.wait_ge(s_up, t * 2 + (u + 1))
                        v.tensor_tensor(hid[:, cols], bank[3 + u][:, 0:256], silu[:, cols], ALU.mult).then_inc(s_h, 1)
                        v.wait_ge(s_hhi, t * 2 + (u + 1))
                        v.tensor_tensor(hT_lo[:, 2 * u:2 * u + 2, :], v3(bank[5][:, 0:256], 2, P),
                                        hT_hi[:, 2 * u:2 * u + 2, :].bitcast(F32), ALU.subtract).then_inc(s_hlo, 1)
                    gathered_lo(t + 1)
                    with v.If(last > 0):
                        split_lo(0, range(PARTS // 2, PARTS), set_no * (3 * PARTS) + 3 * PARTS)
                        for c in (1, 2):
                            split_lo(c, range(PARTS), set_no * (3 * PARTS) + 3 * PARTS)

        @block.tensor
        def _(pe):
            def transposes(dst, src, c, done):
                for k in range(4):
                    last = pe.transpose(dst[:, k * P:(k + 1) * P], src[:, (4 * c + k) * P:(4 * c + k + 1) * P], ident[:])
                last.then_inc(done, 1)

            def products(dst, xs, ws, first, last):
                pe.matmul(dst, xs[0], ws[0], start=first, stop=False)
                pe.matmul(dst, xs[0], ws[1], start=False, stop=False)
                return pe.matmul(dst, xs[1], ws[0], start=False, stop=last)

            pe.wait_ge(s_const, 12)
            pe.wait_ge(s_rw, 32)
            def ctx_step(t):
                t = t.lag(2)
                if t.real():
                    pe.wait_ge(s_round, t.count(1, 2 * BT, 1))
                    after(pe, s_qlo, t.count(2, 4 * BT))
                    for c in range(2):
                        transposes(bank[c], quot[t.n], c, s_qT)

            def tok_step(t):
                z = t.lag(1)
                if z.real():
                    pe.wait_ge(s_back, z.count(1, BT, 1))
                    pe.wait_ge(s_qlo, z.count(2, 4 * BT, 2 * BT))
                    for c in range(2):
                        transposes(bank[c], quot[z.n], c, s_qT)
                y = t.lag(3)
                if y.real():
                    pe.wait_ge(s_norm, y.count(1, BT, 1))
                    after(pe, s_nTs, y.count(2, 2 * BT))
                    for c in range(2):
                        transposes(bank[2 + c], wide(3), c, s_nT)
                y = t.lag(4)
                if y.real():
                    pe.wait_ge(s_nTs, y.count(2, 2 * BT, 2))
                    after(pe, s_logit_s, y.count(1, BT))
                    for k in range(KB):
                        last = pe.matmul(bank[4][:, 0:E], wide(5)[:, k * P:(k + 1) * P], rw[:, k, :], start=k == 0, stop=k == KB - 1)
                    last.then_inc(s_logit, 1)
                if z.real():
                    pe.wait_ge(s_qlo, z.count(2, 4 * BT, 2 * BT + 2))
                    after(pe, s_x1, z.count(1, BT))
                    for h in range(2):
                        cols = slice(512 * h, 512 * h + 512)
                        for k in range(KB):
                            last = products(bank[6 + h][:], (xT_hi[:, k, :], xT_lo[:, k, :]),
                                            (ctxT_hi[:, k, cols], ctxT_lo[:, k, cols]), k == 0, k == KB - 1)
                    last.then_inc(s_prod, 1)

            phase_a(pe, ctx_step, tok_step)

            pe.wait_ge(s_sel, 1)
            for n, m in ((0, tri), (2, ones)):
                for c in range(2):
                    pe.matmul(bank[n + c][:], m[:], sel_e[:, 512 * c:512 * c + 512], start=True, stop=True).then_inc(s_count, 1)

            def gathered(n, k, rows):
                pe.wait_ge(s_gath[n], rows)
                for c in range(2):
                    transposes(bank[c], row_in_t[n], c, s_xT)

            w_of = lambda c, n: tuple(w[:, c, :].rearrange("p (k n) -> p k n", n=n) for w in (w_hi, w_lo))
            pe.wait_ge(s_slots, 1)
            gathered(0, 0, 16)
            pe.wait_ge(s_meta, 16)
            with pe.Fori(0, NT // 2) as it:
                for n in range(2):
                    t = it * 2 + n
                    set_no = pe.value_load(tile_row[0:1, 0, bass.ds(t, 1)], min_val=0, max_val=NE - 1)
                    pe.wait_ge(s_xlo, t * 2 + 2)
                    pe.wait_ge(s_wlo, set_no * (3 * PARTS) + 1 * PARTS)
                    hi, lo = w_of(0, I)
                    for k in range(KB):
                        last = products(bank[2][:], (xT_hi[:, k, :], xT_lo[:, k, :]), (hi[:, k, :], lo[:, k, :]), k == 0, k == KB - 1)
                    last.then_inc(s_gate, 1)
                    pe.wait_ge(s_wlo, set_no * (3 * PARTS) + 2 * PARTS)
                    hi, lo = w_of(1, I)

                    def hidden(u):
                        pe.wait_ge(s_h, t * 2 + (u + 1))
                        pe.wait_ge(s_hlo, t * 2 + u)
                        for m in range(2):
                            last = pe.transpose(bank[5][:, m * P:(m + 1) * P], hid[:, (2 * u + m) * P:(2 * u + m + 1) * P], ident[:])
                        last.then_inc(s_hT, 1)

                    for u in range(2):
                        cols = slice(256 * u, 256 * u + 256)
                        for k in range(KB):
                            if u == 1 and k == KB - 2:
                                hidden(0)
                            last = products(bank[3 + u][:, 0:256], (xT_hi[:, k, :], xT_lo[:, k, :]),
                                            (hi[:, k, cols], lo[:, k, cols]), k == 0, k == KB - 1)
                        last.then_inc(s_up, 1)
                    gathered(1 - n, t + 1, it * 16 + (16 + 16 * n))
                    hidden(1)
                    pe.wait_ge(s_wlo, set_no * (3 * PARTS) + 3 * PARTS)
                    pe.wait_ge(s_y, t * 2)
                    hi, lo = w_of(2, H)
                    for u in range(2):
                        pe.wait_ge(s_hlo, t * 2 + (u + 1))
                        for h in range(2):
                            cols = slice(512 * h, 512 * h + 512)
                            for m in (2 * u, 2 * u + 1):
                                last = products(bank[6 + h][:], (hT_hi[:, m, :], hT_lo[:, m, :]),
                                                (hi[:, m, cols], lo[:, m, cols]), m == 0, m == IB - 1)
                            if u == 1:
                                last.then_inc(s_down, 1)


_INS = ['x', 'ctx_2048', 'L0_ffn_router_w', 'L0_ffn_router_bias', 'L0_ffn_w_gate', 'L0_ffn_w_up', 'L0_ffn_w_down',
        'L0_ffn_sw_gate', 'L0_ffn_sw_up', 'L0_ffn_sw_down']


def kernel(**inputs):
    import numpy as _np
    import concourse.bacc as _bacc
    from concourse import mybir as _mybir
    from concourse.bass_utils import run_bass_kernel_spmd as _run

    nc = _bacc.Bacc("TRN2", target_bir_lowering=False, num_devices=1)
    arrays, args = {}, []
    for name in _INS:
        a = _np.ascontiguousarray(inputs[name])
        arrays[f"in_{name}_dram"] = a
        args.append(nc.dram_tensor(f"in_{name}_dram", a.shape, _mybir.dt.from_np(a.dtype), kind="ExternalInput").ap())
    args.append(nc.dram_tensor("out_0_dram", (T + P, H), F32, kind="ExternalOutput").ap())
    xattn_moe_program(nc, *args)
    r = _run(nc, [arrays], core_ids=[0])
    return r.results[0]["out_0_dram"][:T].reshape(B, S, H)
```

```python
import concourse.bass as bass
from concourse import mybir
from contextlib import ExitStack

F32 = mybir.dt.float32
F32R = mybir.dt.float32r
BF16 = mybir.dt.bfloat16
I32 = mybir.dt.int32
U32 = mybir.dt.uint32
U16 = mybir.dt.uint16
ALU = mybir.AluOpType
ACT = mybir.ActivationFunctionType
AX_X = mybir.AxisListType.X
RMAX = bass.bass_isa.ReduceOp.max

P = 128
B, S, H = 4, 1024, 1024
T = B * S
TT = T // P
BT = S // P
KB = H // P
E, G, TOPG, TOPK = 32, 8, 4, 8
EG = E // G
I = 512
IB = I // P
SH = 2
LN_EPS, ACT_EPS, W_EPS, FP8_MAX = 1e-5, 1e-4, 1e-6, 448.0
ROUTED_SCALE = 2.5
SHT = SH * TT
RT = (T * TOPK + (P - 1) * E) // P + 1
NT = SHT + RT
LT = NT + 3
NE = SH + E
CH = KB * I
PARTS = 4
CP = CH // PARTS
MT = 3 * P
MAGIC = 1.5 * 2.0 ** 23
LOG2E, LN2_HI, LN2_LO = 1.4426950408889634, 0.693145751953125, 1.42860677e-06
EXP_C = [1.0, 1 / 2, 1 / 6, 1 / 24, 1 / 120, 1 / 720, 1 / 5040]
TAKEN = -3.0e38
ROUTE_STEPS = 20
COUNT_TILE = 14
COUNT_PAIR = COUNT_TILE // 2
assert NT % 2 == 0 and NT <= MT - 1 and IB * H == CH


def xattn_moe_program(nc, x, ctx_in, router_w, router_b, w_gate, w_up, w_down, sw_gate, sw_up, sw_down, out):
    x_rows = x.rearrange("b s h -> (b s) h")
    ctx_rows = ctx_in.rearrange("b s h -> (b s) h")
    tokens = nc.dram_tensor("tokens", [T + P, H], F32, kind="Internal").ap()
    slots = nc.dram_tensor("slots", [P * LT, 2], I32, kind="Internal").ap()
    tile_sets = nc.dram_tensor("tile_sets", [2, MT], I32, kind="Internal").ap()

    with ExitStack() as stack:
        def sb(name, shape, dt=F32):
            return stack.enter_context(nc.sbuf_tensor(name, shape, dt))

        def sem(name):
            return stack.enter_context(nc.semaphore(name))

        w_hi = sb("w_hi", [P, 3, CH], F32R)
        w_lo = sb("w_lo", [P, 3, CH], F32R)
        w_raw = sb("w_raw", [P, 3, CH])
        xT_hi = sb("xT_hi", [P, KB, P], F32R)
        xT_lo = sb("xT_lo", [P, KB, P], F32R)
        hT_hi = sb("hT_hi", [P, IB, P], F32R)
        hT_lo = sb("hT_lo", [P, IB, P], F32R)
        row_out = sb("row_out", [P, 2, H])
        row_out_t = [row_out[:, n, :] for n in range(2)]
        scr = sb("scr", [P, 7, H])
        row_in_t = [scr[:, 5 + n, :] for n in range(2)]
        silu = sb("silu", [P, I])
        hid = sb("hid", [P, I])
        tile_row = sb("tile_row", [1, 2, MT], I32)
        pairs_i = sb("pairs_i", [P, 1], I32)
        sel_e = sb("sel_e", [P, TT * E], BF16)
        ident = sb("ident", [P, P])
        ident_b = sb("ident_b", [P, P], BF16)
        tri = sb("tri", [P, P], BF16)
        ones = sb("ones", [P, P], BF16)
        rw = sb("rw", [P, KB, E])
        bias = sb("bias", [P, E])
        stats = [sb(f"stats{n}", [P, 2, 6]) for n in range(2)]
        mv = [sb(f"mv{n}", [P, 2]) for n in range(2)]
        sm = [sb(f"sm{n}", [P, 6]) for n in range(2)]
        sd = [sb(f"sd{n}", [P, 1]) for n in range(2)]
        amax = sb("amax", [P, KB])
        amax_c = sb("amax_c", [P, KB])
        amax_all = [sb(f"amax_all{n}", [P, KB]) for n in range(2)]
        cinv = sb("cinv", [P, 2, KB])
        cscale = sb("cscale", [P, BT * KB])
        qscale = [sb(f"qscale{n}", [P, 3, KB]) for n in range(2)]
        ef = sb("ef", [P, 8, E])
        ei = sb("ei", [P, E], I32)
        pick = sb("pick", [P, 2, E])
        top8 = sb("top8", [P, 8])
        token_no = sb("token_no", [P, TT], I32)
        tile_no = sb("tile_no", [P, 3], I32)
        tile_f = sb("tile_f", [P, 2, 3])
        tile_c = sb("tile_c", [P, 3, 3])
        set_i = sb("set_i", [P, 2, 3], I32)
        stage_rows = sb("stage_rows", [P, TOPK], I32)
        stage_picks = sb("stage_picks", [P, 2 * TOPK], I32)
        idx_g = [sb(f"idx_g{n}", [P, 2], I32) for n in range(2)]
        idx_s = [sb(f"idx_s{n}", [P, 2], I32) for n in range(2)]
        bank = [stack.enter_context(nc.psum_tensor(f"bank{n}", [P, 512], F32)) for n in range(8)]

        s_const = sem("s_const")
        s_init = sem("s_init")
        s_rw = sem("s_rw")
        s_cin = [sem("s_cin0"), sem("s_cin1")]
        s_xin = [sem("s_xin0"), sem("s_xin1")]
        s_var = [sem("s_var0"), sem("s_var1")]
        s_sqrt = [sem("s_sqrt0"), sem("s_sqrt1")]
        s_amax = sem("s_amax")
        s_amax_all = sem("s_amax_all")
        s_cinv = sem("s_cinv")
        s_cquot = sem("s_cquot")
        s_cstep = sem("s_cstep")
        s_csum = sem("s_csum")
        s_cround = sem("s_cround")
        s_cT = sem("s_cT")
        s_cqT = sem("s_cqT")
        s_chi = sem("s_chi")
        s_clo = sem("s_clo")
        s_scaled = sem("s_scaled")
        s_zq = sem("s_zq")
        s_round = sem("s_round")
        s_back = sem("s_back")
        s_qT = sem("s_qT")
        s_qhi = sem("s_qhi")
        s_qlo = sem("s_qlo")
        s_prod = sem("s_prod")
        s_x1 = sem("s_x1")
        s_root = sem("s_root")
        s_x1_st = [sem("s_x1_st0"), sem("s_x1_st1")]
        s_norm = sem("s_norm")
        s_norm_st = sem("s_norm_st")
        s_nT = sem("s_nT")
        s_nTs = sem("s_nTs")
        s_logit = sem("s_logit")
        s_logit_s = sem("s_logit_s")
        s_dve = sem("s_dve")
        s_passed = sem("s_passed")
        s_dve_ctx = sem("s_dve_ctx")
        s_dve_cs = sem("s_dve_cs")
        s_dve_q = sem("s_dve_q")
        s_dve_p = sem("s_dve_p")
        s_dve_r = sem("s_dve_r")
        s_sel = sem("s_sel")
        s_count = sem("s_count")
        s_counted = sem("s_counted")
        s_slots = sem("s_slots")
        s_sets = sem("s_sets")
        s_meta_st = sem("s_meta_st")
        s_meta = sem("s_meta")
        s_stage = sem("s_stage")
        s_slot_st = sem("s_slot_st")
        s_raw = [sem(f"s_raw{c}") for c in range(3)]
        s_whi = sem("s_whi")
        s_wlo = sem("s_wlo")
        s_idx_g = [sem("s_idx_g0"), sem("s_idx_g1")]
        s_idx_s = [sem("s_idx_s0"), sem("s_idx_s1")]
        s_gath = [sem("s_gath0"), sem("s_gath1")]
        s_add = [sem("s_add0"), sem("s_add1")]
        s_xT = sem("s_xT")
        s_xhi = sem("s_xhi")
        s_xlo = sem("s_xlo")
        s_gate = sem("s_gate")
        s_up = sem("s_up")
        s_silu = sem("s_silu")
        s_h = sem("s_h")
        s_hT = sem("s_hT")
        s_hhi = sem("s_hhi")
        s_hlo = sem("s_hlo")
        s_down = sem("s_down")
        s_y = sem("s_y")

        block = stack.enter_context(nc.Block())
        v3 = lambda ap, a, b: ap.rearrange("p (a b) -> p a b", a=a, b=b)
        ctxT_hi = w_hi.rearrange("p c n -> p (c n)")[:, CH:CH + KB * S].rearrange("p (k n) -> p k n", k=KB)
        ctxT_lo = w_lo.rearrange("p c n -> p (c n)")[:, CH:CH + KB * S].rearrange("p (k n) -> p k n", k=KB)
        wide = lambda n: scr[:, n, :]
        NP = TT * TOPK
        slot_f = scr[:, 4, 0:NP].rearrange("p (i k) -> p i k", k=TOPK)
        slot_rows = scr[:, 4, NP:2 * NP].bitcast(I32)
        picks = scr[:, 4, 2 * NP:4 * NP].bitcast(I32).rearrange("p (n two) -> p n two", two=2)
        slot_i = scr[:, 0, 0:2 * NP].bitcast(I32).rearrange("p (a n) -> p a n", a=2)
        raw_rows = w_raw.rearrange("p c n -> p (c n)").rearrange("p (r n) -> p r n", n=H)
        cin = raw_rows[:, 0:4, :].rearrange("p r n -> p (r n)")
        xin = raw_rows[:, 4:8, :].rearrange("p r n -> p (r n)")
        quot = [raw_rows[:, 8 + n, :] for n in range(2)]
        step = raw_rows[:, 10, 0:H // 2].bitcast(BF16)
        cstep = raw_rows[:, 11, 0:H // 2].bitcast(BF16)
        cq = sel_e
        qT = scr[:, 3:7, :].rearrange("p r n -> p (r n)").bitcast(BF16)

        def ring(buf, t):
            at = ((t.q * 2 + t.off % 4) % 4) * H
            return buf[:, bass.ds(at, H)]

        class At:

            def __init__(self, b, q, off):
                self.bv, self.bo = b
                self.q, self.off = q, off
                self.n = off % 2

            def lag(self, n):
                return At((self.bv, self.bo), self.q, self.off - n)

            def next_batch(self):
                return At((self.bv, self.bo + 1), self.q, self.off)

            def real(self):
                return not isinstance(self.bv, int) or 0 <= self.bo * BT + self.off < TT

            def count(self, per=1, more=0):
                return self.bv * (BT * per) + self.q * (2 * per) + ((self.bo * BT + self.off) * per + more)

            def half(self, per, more=0):
                return self.bv * (BT // 2 * per) + self.q * per + ((self.bo * (BT // 2) + self.off // 2) * per + more)

            def batch(self, per, more=0):
                return self.bv * per + ((self.bo + self.off // BT) * per + more)

            def within(self, per):
                return self.q * (2 * per) + (self.off % BT) * per

        def after(eng, s, n):
            if not isinstance(n, int) or n > 0:
                eng.wait_ge(s, n)

        def first_batch(c):
            return isinstance(c.bv, int) and c.bo * BT + c.off < BT

        def phase_a(eng, step_of):
            def batch(b):
                for j in range(4):
                    step_of(At(b, 0, j))
                with eng.Fori(0, 2) as q:
                    step_of(At(b, q, 4))
                    step_of(At(b, q, 5))

            batch((0, -1))
            batch((0, 0))
            with eng.Fori(0, B - 2) as b:
                batch((b, 1))
            batch((0, B - 1))
            for j in range(4):
                step_of(At((0, B), 0, j))

        @block.sync
        def _(sp):
            sp.dma_start(rw[:], router_w.rearrange("(k p) e -> p k e", p=P)).then_inc(s_rw, 16)
            sp.dma_start(bias[:], router_b.partition_broadcast(P)).then_inc(s_rw, 16)
            def loads(t):
                c = t.next_batch()
                if c.real():
                    after(sp, s_cround, c.count(1, -3))
                    sp.sem_inc(s_passed)
                    after(sp, s_cin[c.n], c.half(16))
                    sp.sem_inc(s_passed)
                    sp.dma_start(ring(cin, c), ctx_rows[bass.ds(c.count(P), P), :]).then_inc(s_cin[c.n], 16)
                if t.real():
                    after(sp, s_x1, t.count(1, -3))
                    sp.sem_inc(s_passed)
                    after(sp, s_xin[t.n], t.half(16))
                    sp.sem_inc(s_passed)
                    sp.dma_start(ring(xin, t), x_rows[bass.ds(t.count(P), P), :]).then_inc(s_xin[t.n], 16)

            phase_a(sp, loads)
            def chunk(c, s):
                return w_raw[:, c, :].rearrange("p (k n) -> p k n", n=s)

            for s in range(SH):
                for c, src in enumerate((sw_gate, sw_up, sw_down)):
                    if s == 0:
                        sp.wait_ge(*((s_cround, TT), (s_x1, TT), (s_qT, 2 * TT))[c])
                    else:
                        sp.wait_ge(s_wlo, PARTS * (3 * (s - 1) + c + 1))
                    if c < 2:
                        sp.dma_start(chunk(c, I), src[:, s * I:(s + 1) * I].rearrange("(k p) n -> p k n", p=P)).then_inc(s_raw[c], 16)
                    else:
                        sp.dma_start(chunk(c, H), src[s * I:(s + 1) * I, :].rearrange("(k p) n -> p k n", p=P)).then_inc(s_raw[c], 16)
            with sp.Fori(0, E) as e:
                for c, src in enumerate((w_gate, w_up, w_down)):
                    sp.wait_ge(s_wlo, e * (3 * PARTS) + PARTS * (3 * (SH - 1) + c + 1))
                    rows = src.rearrange("e k n -> (e k) n")[bass.ds(e * src.shape[1], src.shape[1]), :]
                    sp.dma_start(chunk(c, src.shape[2]), rows.rearrange("(k p) n -> p k n", p=P)).then_inc(s_raw[c], 16)

        @block.gpsimd
        def _(pool):
            pool.memset(ident[:], 0.0).then_inc(s_const, 1)
            pool.memset(ident_b[:], 0.0).then_inc(s_const, 1)
            pool.memset(tri[:], 1.0).then_inc(s_const, 1)
            pool.memset(ones[:], 1.0).then_inc(s_const, 1)
            pool.memset(wide(0), 0.0).then_inc(s_const, 1)
            table = scr[:, 1, 0:2 * LT].bitcast(I32).rearrange("p (t two) -> p t two", two=2)
            weight = scr[:, 1, 0:2 * LT].rearrange("p (t two) -> p t two", two=2)
            pool.iota(table[:, 0:SHT, 0:1], [[0, SH], [P, TT], [0, 1]], base=0, channel_multiplier=1).then_inc(s_const, 1)
            pool.iota(table[:, SHT:LT, 0:1], [[0, LT - SHT], [0, 1]], base=T, channel_multiplier=1).then_inc(s_const, 1)
            pool.memset(weight[:, 0:SHT, 1:2], 1.0).then_inc(s_const, 1)
            pool.memset(weight[:, SHT:LT, 1:2], 0.0).then_inc(s_const, 1)
            pool.iota(tile_row[:, 0, 0:SHT].rearrange("o (s t) -> o s t", s=SH), [[1, SH], [0, TT]], base=0, channel_multiplier=0).then_inc(s_const, 1)
            pool.memset(tile_row[:, 1, 0:SHT], 0).then_inc(s_const, 1)
            pool.iota(token_no[:], [[P, TT]], base=0, channel_multiplier=1).then_inc(s_const, 1)
            pool.iota(tile_no[:], [[P, 3]], base=0, channel_multiplier=1).then_inc(s_const, 1)
            pool.wait_ge(s_const, 13)
            for s in range(SH):
                pool.memset(tile_row[:, 1, (s + 1) * TT - 1:(s + 1) * TT], 1).then_inc(s_const, 1)
            pool.affine_select(out=ident[:], in_=ident[:], compare_op=ALU.not_equal, fill=1.0,
                               base=0, pattern=[[-1, P]], channel_multiplier=1).then_inc(s_const, 1)
            pool.affine_select(out=ident_b[:], in_=ident_b[:], compare_op=ALU.not_equal, fill=1.0,
                               base=0, pattern=[[-1, P]], channel_multiplier=1).then_inc(s_const, 1)
            pool.affine_select(out=tri[:], in_=tri[:], compare_op=ALU.is_gt, fill=0.0,
                               base=0, pattern=[[1, P]], channel_multiplier=-1).then_inc(s_const, 1)
            pool.dma_start(slots.rearrange("(p t) two -> p (t two)", p=P), scr[:, 1, 0:2 * LT].bitcast(I32)).then_inc(s_init, 16)
            pool.dma_start(tokens[T:T + P, :], wide(0)).then_inc(s_init, 16)
            pool.dma_start(out[T:T + P, :], wide(0)).then_inc(s_init, 16)
            pool.wait_ge(s_init, 48)

            def pool_step(t):
                c = t.next_batch()
                if c.real():
                    pool.wait_ge(s_amax, c.count(1, 1))
                    after(pool, s_cinv, c.count(1, -1))
                    pool.sem_inc(s_passed)
                    pool.partition_all_reduce(amax_all[c.n][:], amax_c[:], P, RMAX).then_inc(s_amax_all, 1)
                c = c.lag(1)
                if c.real():
                    row = ring(cin, c)
                    pool.wait_ge(s_cstep, c.count(1, 1))
                    pool.sem_inc(s_passed)
                    pool.tensor_tensor(row, row, cstep, ALU.add).then_inc(s_csum, 1)
                    if not first_batch(c):
                        pool.wait_ge(s_csum, c.count(1, 1))
                        after(pool, s_cT, c.count(1))
                        pool.sem_inc(s_passed)
                        pool.tensor_tensor(cq[:], row, cstep, ALU.subtract).then_inc(s_cround, 1)
                z = t.lag(3)
                if z.real():
                    pool.wait_ge(s_norm, z.count(1, 1))
                    pool.sem_inc(s_passed)
                    pool.dma_start(tokens[bass.ds(z.count(P), P), :], wide(1)).then_inc(s_norm_st, 16)
                if t.real():
                    pool.wait_ge(s_scaled, t.count(1, 1))
                    pool.tensor_tensor(quot[t.n], quot[t.n], step, ALU.add).then_inc(s_zq, 1)
                    pool.wait_ge(s_zq, t.count(1, 1))
                    pool.tensor_tensor(quot[t.n], quot[t.n], step, ALU.subtract).then_inc(s_round, 1)
                z = t.lag(2)
                if z.real():
                    pool.wait_ge(s_x1, z.count(1, 1))
                    pool.sem_inc(s_passed)
                    pool.dma_start(out[bass.ds(z.count(P), P), :], row_out_t[z.n]).then_inc(s_x1_st[z.n], 16)

            phase_a(pool, pool_step)
            slot_tiles = slots.rearrange("(p t) two -> p t two", p=P)

            def load_idx(dst, t, done):
                pool.dma_start(dst[:], slot_tiles[:, bass.ds(t, 1), :].rearrange("p t two -> p (t two)")).then_inc(done, 16)

            def gather(n):
                pool.indirect_dma_start(out=row_in_t[n], out_offset=None, in_=tokens[:, :],
                                        in_offset=bass.IndirectOffsetOnAxis(ap=idx_g[n][:, 0:1].bitcast(U32), axis=0)).then_inc(s_gath[n], 16)

            def tile_step(it, n):
                pool.wait_ge(s_idx_g[n], it * 16 + 32)
                pool.wait_ge(s_xT, it * 4 + (2 * n + 2))
                pool.sem_inc(s_passed)
                gather(n)
                pool.wait_ge(s_gath[1 - n], it * 16 + (16 + 16 * n))
                pool.sem_inc(s_passed)
                if n == 0:
                    load_idx(idx_g[1], it * 2 + 3, s_idx_g[1])
                else:
                    load_idx(idx_g[0], it * 2 + 4, s_idx_g[0])
                pool.wait_ge(s_y, it * 4 + (2 * n + 2))
                if n == 0:
                    pool.wait_ge(s_add[1], it * 16)
                else:
                    pool.wait_ge(s_add[0], it * 16 + 16)
                pool.sem_inc(s_passed)
                pool.indirect_dma_start(out=out[:, :], out_offset=bass.IndirectOffsetOnAxis(ap=idx_s[n][:, 0:1].bitcast(U32), axis=0),
                                        in_=row_out_t[n], in_offset=None, compute_op=ALU.add).then_inc(s_add[n], 16)
                pool.wait_ge(s_add[n], it * 16 + 16)
                pool.sem_inc(s_passed)
                load_idx(idx_s[n], it * 2 + (n + 2), s_idx_s[n])

            for n in range(2):
                load_idx(idx_g[n], n, s_idx_g[n])
                load_idx(idx_s[n], n, s_idx_s[n])
            for n in range(2):
                pool.wait_ge(s_x1_st[n], 16 * (TT // 2))
            pool.wait_ge(s_norm_st, 16 * TT)
            for n in range(2):
                pool.wait_ge(s_idx_g[n], 16)
                gather(n)
            pool.wait_ge(s_gath[0], 16)
            load_idx(idx_g[0], 2, s_idx_g[0])

            first = ROUTE_STEPS // 2 + 1
            with pool.Fori(0, first) as it:
                for n in range(2):
                    tile_step(it, n)
            pool.wait_ge(s_sets, 1)
            for d in range(2):
                with nc.allow_non_contiguous_dma(reason="three values per partition"):
                    pool.dma_start(tile_sets[d:d + 1, :].rearrange("a (c p) -> p (a c)", p=P), set_i[:, d, :]).then_inc(s_meta_st, 16)
            pool.wait_ge(s_meta_st, 32)
            pool.dma_start(tile_row[:, :, SHT:MT], tile_sets[:, SHT:MT].rearrange("(o d) m -> o d m", o=1)).then_inc(s_meta, 16)
            pool.wait_ge(s_slots, 1)
            with pool.Fori(0, TT // 2) as i:
                for h in range(2):
                    after(pool, s_slot_st, i * (32 * TOPK) + h * (16 * TOPK))
                    pool.tensor_copy(stage_rows[:], slot_rows[:, bass.ds(i * (2 * TOPK) + h * TOPK, TOPK)]).then_inc(s_stage, 1)
                    pool.tensor_copy(stage_picks[:], picks.rearrange("p n two -> p (n two)")[:, bass.ds(i * (4 * TOPK) + h * (2 * TOPK), 2 * TOPK)]).then_inc(s_stage, 1)
                    pool.wait_ge(s_stage, i * 4 + (2 * h + 2))
                    pool.sem_inc(s_passed)
                    for k in range(TOPK):
                        pool.indirect_dma_start(out=slots[:, :], out_offset=bass.IndirectOffsetOnAxis(ap=stage_rows[:, k:k + 1].bitcast(U32), axis=0),
                                                in_=stage_picks[:, 2 * k:2 * k + 2], in_offset=None).then_inc(s_slot_st, 16)
                    tile_step(i + first, h)
            with pool.Fori(first + TT // 2, SHT // 2 - 2) as it:
                for n in range(2):
                    tile_step(it, n)
            pool.wait_ge(s_slot_st, 16 * TOPK * TT)
            pairs = pool.value_load(pairs_i[0:1, 0:1], min_val=SHT // 2 + 1, max_val=NT // 2)
            with pool.Fori(SHT // 2 - 2, NT // 2) as it:
                with pool.If(it < pairs):
                    for n in range(2):
                        tile_step(it, n)
            for s, more in ((s_add[0], 0), (s_add[1], 0), (s_idx_g[0], 32), (s_idx_g[1], 16), (s_idx_s[0], 16), (s_idx_s[1], 16), (s_gath[0], 16), (s_gath[1], 16)):
                pool.wait_ge(s, pairs * 16 + more)
                pool.sem_inc(s_passed)

        @block.scalar
        def _(act):
            def root(k, t):
                act.wait_ge(s_var[k], t.count(1, 1))
                act.activation(sd[k][:], sm[k][:, 0:1], ACT.Sqrt).then_inc(s_sqrt[k], 1)

            def split_hi(c, loaded, parts=range(PARTS)):
                act.wait_ge(s_raw[c], loaded)
                for s in parts:
                    part = slice(s * CP, (s + 1) * CP)
                    act.activation(w_hi[:, c, part], w_raw[:, c, part], ACT.Copy).then_inc(s_whi, 1)

            def context_hi(t, h):
                after(act, s_prod, t.batch(2 * BT, h - 1))
                after(act, s_cqT, t.batch(BT, BT // 2 * (h + 1)))
                for k in range(KB):
                    for i in range(4 * h, 4 * h + 4):
                        ins = act.activation(ctxT_hi[:, k, i * P:(i + 1) * P], qT[:, (i * KB + k) * P:(i * KB + k + 1) * P],
                                             ACT.Copy, scale=cscale[:, i * KB + k:i * KB + k + 1])
                    ins.then_inc(s_chi, 1)

            def context_quotient(c):
                if c.real():
                    act.wait_ge(s_cinv, c.count(1, 1))
                    for k in range(KB):
                        part = ring(cin, c)[:, k * P:(k + 1) * P]
                        ins = act.activation(part, part, ACT.Copy, scale=cinv[:, 1, k:k + 1])
                    ins.then_inc(s_cquot, 1)

            def act_step(t):
                c = t.next_batch()
                if t.real():
                    root(0, t)
                z = t.lag(3)
                if z.real():
                    act.wait_ge(s_root, z.count(1, 1))
                    after(act, s_norm_st, z.count(16))
                    after(act, s_nT, z.count(2))
                    act.activation(wide(1), row_out_t[z.n], ACT.Identity, bias=sm[1][:, 5:6], scale=sm[1][:, 4:5]).then_inc(s_norm, 1)
                if c.off != 0:
                    context_quotient(c)
                z = t.lag(1)
                if z.real():
                    after(act, s_prod, z.count(2))
                    for h in range(2):
                        act.wait_ge(s_qT, z.count(2, h + 1))
                        act.activation(xT_hi[:, 4 * h:4 * h + 4, :], v3(bank[h][:], 4, P), ACT.Copy).then_inc(s_qhi, 1)
                z = t.lag(4)
                if z.real():
                    act.wait_ge(s_logit, z.count(1, 1))
                    act.activation(wide(0)[:, bass.ds(z.count(E), E)], bank[4][:, 0:E], ACT.Copy).then_inc(s_logit_s, 1)
                z = t.lag(3)
                if z.real():
                    after(act, s_logit, z.count(1))
                    for h in range(2):
                        act.wait_ge(s_nT, z.count(2, h + 1))
                        act.activation(wide(2)[:, h * 512:(h + 1) * 512], bank[2 + h][:], ACT.Copy).then_inc(s_nTs, 1)
                z = c.lag(2)
                if z.real():
                    act.wait_ge(s_cT, z.count(1, 1))
                    after(act, s_clo, z.batch(2 * KB))
                    act.activation(qT[:, bass.ds(z.within(H), H)], bank[5][:].bitcast(BF16), ACT.Copy).then_inc(s_cqT, 1)
                if t.real() and t.off == 1:
                    context_hi(t, 1)
                z = t.lag(2)
                if z.real():
                    root(1, z)
                if t.real():
                    act.wait_ge(s_round, t.count(1, 1))
                    for k in range(KB):
                        ins = act.activation(quot[t.n][:, k * P:(k + 1) * P], quot[t.n][:, k * P:(k + 1) * P], ACT.Copy, scale=qscale[t.n][:, 2, k:k + 1])
                    ins.then_inc(s_back, 1)
                if t.real() and t.off == 0:
                    context_hi(t, 0)
                if c.off == 0:
                    context_quotient(c)
                if isinstance(t.bv, int) and t.bo == B:
                    split_hi(0, 16, [t.off])

            phase_a(act, act_step)

            def gathered_hi(k):
                for c in range(2):
                    act.wait_ge(s_xT, k * 2 + (c + 1))
                    act.activation(xT_hi[:, 4 * c:4 * c + 4, :], v3(bank[c][:], 4, P), ACT.Copy).then_inc(s_xhi, 1)

            act.wait_ge(s_prod, 2 * TT)
            for c in (1, 2):
                split_hi(c, 16)
            gathered_hi(0)

            def tile(it, n):
                t = it * 2 + n
                last = act.value_load(tile_row[0:1, 1, bass.ds(t, 1)], min_val=0, max_val=1)
                set_no = act.value_load(tile_row[0:1, 0, bass.ds(t, 1)], min_val=0, max_val=NE - 1)
                act.wait_ge(s_gate, t + 1)
                act.wait_ge(s_h, t * 2)
                act.activation(silu[:], bank[2][:], ACT.Silu).then_inc(s_silu, 1)
                with act.If(last > 0):
                    split_hi(0, set_no * 16 + 32)
                for u in range(2):
                    act.wait_ge(s_hT, t * 2 + (u + 1))
                    act.activation(hT_hi[:, 2 * u:2 * u + 2, :], v3(bank[5][:, 0:256], 2, P), ACT.Copy).then_inc(s_hhi, 1)
                act.wait_ge(s_up, t * 2 + 2)
                gathered_hi(t + 1)
                with act.If(last > 0):
                    split_hi(1, set_no * 16 + 32)
                    act.wait_ge(s_down, t * 2 + 2)
                    split_hi(2, set_no * 16 + 32)
                for c in range(2):
                    act.wait_ge(s_down, t * 2 + (c + 1))
                    if c == 0:
                        act.wait_ge(s_idx_s[n], it * 16 + 16)
                        if n == 0:
                            act.wait_ge(s_add[0], it * 16)
                        else:
                            act.wait_ge(s_add[1], it * 16)
                    act.activation(row_out_t[n][:, c * 512:(c + 1) * 512], bank[6 + c][:], ACT.Copy,
                                   scale=idx_s[n][:, 1:2].bitcast(F32)).then_inc(s_y, 1)

            with act.Fori(0, SHT // 2) as it:
                for n in range(2):
                    tile(it, n)
            act.wait_ge(s_meta, 16)
            pairs = act.value_load(pairs_i[0:1, 0:1], min_val=SHT // 2 + 1, max_val=NT // 2)
            with act.Fori(SHT // 2, NT // 2) as it:
                with act.If(it < pairs):
                    for n in range(2):
                        tile(it, n)

        @block.vector
        def _(v):
            chain = [None, 0, 0]

            def start(s, before):
                chain[:] = [s, before, 0]

            def link(ins):
                chain[2] += 1
                ins.then_inc(chain[0], 1)
                v.wait_ge(chain[0], chain[1] + chain[2])

            def moments(src, k):
                v.bn_stats(stats[k][:, 0, :], src[:, 0:512])
                link(v.bn_stats(stats[k][:, 1, :], src[:, 512:1024]))
                v.sem_inc(s_passed)
                link(v.bn_aggr(mv[k][:], stats[k].rearrange("p a b -> p (a b)")))
                v.tensor_scalar(sm[k][:, 0:1], mv[k][:, 1:2], LN_EPS, None, ALU.add).then_inc(s_var[k], 1)

            def inverse_root(k):
                m = sm[k]
                link(v.reciprocal(m[:, 1:2], sd[k][:]))
                link(v.scalar_tensor_tensor(m[:, 2:3], m[:, 1:2], m[:, 0:1], m[:, 1:2], ALU.mult, ALU.mult))
                link(v.tensor_scalar(m[:, 3:4], m[:, 2:3], -0.5, 1.5, ALU.mult, ALU.add))
                link(v.tensor_tensor(m[:, 4:5], m[:, 3:4], m[:, 1:2], ALU.mult))

            def rounding_step(dst, src):
                upper = src.bitcast(U16).rearrange("p (n two) -> p n two", two=2)[:, :, 1]
                link(v.tensor_scalar(dst.bitcast(U16), upper, 0x7F80, None, ALU.bitwise_and))
                return v.tensor_scalar(dst, dst, 2.0 ** -6, 1.5 * 2.0 ** 20, ALU.max, ALU.mult)

            K_CS, K_C, K_Q, K_P, K_R = 1, 2, 13, 2, 4

            def split_lo(c, parts, before):
                for s in parts:
                    part = slice(s * CP, (s + 1) * CP)
                    v.wait_ge(s_whi, before + (c * PARTS + s + 1))
                    v.tensor_tensor(w_lo[:, c, part], w_raw[:, c, part], w_hi[:, c, part].bitcast(F32), ALU.subtract).then_inc(s_wlo, 1)

            def context_lo(t, h):
                for k in range(KB):
                    v.wait_ge(s_chi, t.batch(2 * KB, KB * h + k + 1))
                    for i in range(4 * h, 4 * h + 4):
                        ins = v.scalar_tensor_tensor(ctxT_lo[:, k, i * P:(i + 1) * P], qT[:, (i * KB + k) * P:(i * KB + k + 1) * P],
                                                     cscale[:, i * KB + k:i * KB + k + 1], ctxT_hi[:, k, i * P:(i + 1) * P].bitcast(F32),
                                                     ALU.mult, ALU.subtract)
                    ins.then_inc(s_clo, 1)

            def context_scales(c):
                if c.real():
                    start(s_dve_ctx, c.count(K_C))
                    v.wait_ge(s_amax_all, c.count(1, 1))
                    link(v.tensor_scalar(cinv[:, 0, :], amax_all[c.n][:], W_EPS, None, ALU.max))
                    link(v.reciprocal(cinv[:, 1, :], cinv[:, 0, :]))
                    v.tensor_scalar(cscale[:, bass.ds(c.within(KB), KB)], cinv[:, 0, :], 1.0 / FP8_MAX, None, ALU.mult)
                    v.tensor_scalar(cinv[:, 1, :], cinv[:, 1, :], FP8_MAX, None, ALU.mult).then_inc(s_cinv, 1)
                    assert chain[2] == K_C, chain

            def context_rounded(z):
                v.wait_ge(s_csum, z.count(1, 1))
                after(v, s_cT, z.count(1))
                v.tensor_tensor(cq[:], ring(cin, z), cstep, ALU.subtract).then_inc(s_cround, 1)

            def dve_step(t):
                c = t.next_batch()
                if c.real():
                    v.wait_ge(s_cin[c.n], c.half(16, 16))
                    after(v, s_amax_all, c.count(1))
                    v.tensor_reduce(amax_c[:], v3(ring(cin, c), KB, P), AX_X, ALU.max, apply_absolute_value=True).then_inc(s_amax, 1)
                z = c.lag(2)
                if z.real() and first_batch(z) and z.off != -1:
                    context_rounded(z)
                z = c.lag(1)
                if z.real():
                    start(s_dve_cs, z.count(K_CS))
                    v.wait_ge(s_cquot, z.count(1, 1))
                    after(v, s_cround, z.count(1))
                    rounding_step(cstep, ring(cin, z)).then_inc(s_cstep, 1)
                    assert chain[2] == K_CS, chain
                    if first_batch(z) and z.off == -1:
                        context_rounded(z)
                if t.real():
                    start(s_dve_q, t.count(K_Q))
                    v.wait_ge(s_xin[t.n], t.half(16, 16))
                    moments(ring(xin, t), 0)
                    mine = list(chain)
                if c.off != 0:
                    context_scales(c)
                z = t.lag(3)
                if z.real():
                    start(s_dve_r, z.count(K_R))
                    v.wait_ge(s_sqrt[1], z.count(1, 1))
                    after(v, s_norm, z.count(1))
                    inverse_root(1)
                    v.scalar_tensor_tensor(sm[1][:, 5:6], mv[1][:, 0:1], -1.0, sm[1][:, 4:5], ALU.mult, ALU.mult).then_inc(s_root, 1)
                    assert chain[2] == K_R, chain
                if t.real():
                    chain[:] = mine
                    q, qs = quot[t.n], qscale[t.n]
                    v.wait_ge(s_sqrt[0], t.count(1, 1))
                    inverse_root(0)
                    after(v, s_qT, t.count(2, -2))
                    link(v.tensor_scalar(q, ring(xin, t), mv[0][:, 0:1], sm[0][:, 4:5], ALU.subtract, ALU.mult))
                    link(v.tensor_reduce(amax[:], v3(q, KB, P), AX_X, ALU.max, apply_absolute_value=True))
                    link(v.tensor_scalar(qs[:, 0, :], amax[:], ACT_EPS, None, ALU.max))
                    link(v.reciprocal(qs[:, 1, :], qs[:, 0, :]))
                    v.tensor_scalar(qs[:, 1, :], qs[:, 1, :], FP8_MAX, None, ALU.mult)
                    link(v.tensor_scalar(qs[:, 2, :], qs[:, 0, :], 1.0 / FP8_MAX, None, ALU.mult))
                    link(v.tensor_tensor(v3(q, KB, P), v3(q, KB, P), qs[:, 1, :].unsqueeze(2).to_broadcast([P, KB, P]), ALU.mult))
                    after(v, s_round, t.count(1))
                    rounding_step(step, q).then_inc(s_scaled, 1)
                    assert chain[2] == K_Q, chain
                z = t.lag(2)
                if z.real():
                    after(v, s_x1_st[z.n], z.half(16))
                    after(v, s_norm, z.count(1, -1))
                    for h in range(2):
                        cols = slice(h * 512, (h + 1) * 512)
                        v.wait_ge(s_prod, z.count(2, h + 1))
                        ins = v.tensor_tensor(row_out_t[z.n][:, cols], bank[6 + h][:], ring(xin, z)[:, cols], ALU.add)
                    ins.then_inc(s_x1, 1)
                y = t.lag(1)
                if y.real():
                    for h in range(2):
                        v.wait_ge(s_qhi, y.count(2, h + 1))
                        v.tensor_tensor(xT_lo[:, 4 * h:4 * h + 4, :], v3(bank[h][:], 4, P),
                                        xT_hi[:, 4 * h:4 * h + 4, :].bitcast(F32), ALU.subtract).then_inc(s_qlo, 1)
                if t.real() and t.off == 1:
                    context_lo(t, 1)
                if z.real():
                    start(s_dve_p, z.count(K_P))
                    v.wait_ge(s_x1, z.count(1, 1))
                    after(v, s_root, z.count(1))
                    moments(row_out_t[z.n], 1)
                    assert chain[2] == K_P, chain
                if t.real() and t.off == 0:
                    context_lo(t, 0)
                if c.off == 0:
                    context_scales(c)
                if isinstance(t.bv, int) and t.bo == B:
                    split_lo(0, [t.off], 0)

            v.wait_ge(s_const, 18)
            phase_a(v, dve_step)

            def gathered_lo(k):
                for c in range(2):
                    v.wait_ge(s_xhi, k * 2 + (c + 1))
                    v.tensor_tensor(xT_lo[:, 4 * c:4 * c + 4, :], v3(bank[c][:], 4, P),
                                    xT_hi[:, 4 * c:4 * c + 4, :].bitcast(F32), ALU.subtract).then_inc(s_xlo, 1)

            def tile(it, n):
                t = it * 2 + n
                early = isinstance(t, int)
                if not early:
                    last = v.value_load(tile_row[0:1, 1, bass.ds(t, 1)], min_val=0, max_val=1)
                    set_no = v.value_load(tile_row[0:1, 0, bass.ds(t, 1)], min_val=0, max_val=NE - 1)
                    with v.If(last > 0):
                        split_lo(0, range(0, PARTS // 2), set_no * (3 * PARTS) + 3 * PARTS)
                v.wait_ge(s_silu, t + 1)
                for u in range(2):
                    cols = slice(256 * u, 256 * u + 256)
                    v.wait_ge(s_up, t * 2 + (u + 1))
                    v.tensor_tensor(hid[:, cols], bank[3 + u][:, 0:256], silu[:, cols], ALU.mult).then_inc(s_h, 1)
                    v.wait_ge(s_hhi, t * 2 + (u + 1))
                    v.tensor_tensor(hT_lo[:, 2 * u:2 * u + 2, :], v3(bank[5][:, 0:256], 2, P),
                                    hT_hi[:, 2 * u:2 * u + 2, :].bitcast(F32), ALU.subtract).then_inc(s_hlo, 1)
                gathered_lo(t + 1)
                if not early:
                    with v.If(last > 0):
                        split_lo(0, range(PARTS // 2, PARTS), set_no * (3 * PARTS) + 3 * PARTS)
                        for c in (1, 2):
                            split_lo(c, range(PARTS), set_no * (3 * PARTS) + 3 * PARTS)
                    v.sem_inc(s_passed)

            tte = lambda n: wide(n).rearrange("p (i e) -> p i e", e=E)
            eti = lambda n: wide(n).rearrange("p (e i) -> p e i", i=TT)
            four = wide(1).rearrange("p (q m) -> p q m", m=EG)
            q4 = lambda n, m: wide(n)[:, 256 * m:256 * m + 256]

            def scores_1():
                start(s_dve, 0)
                v.wait_ge(s_logit_s, TT)
                v.wait_ge(s_rw, 32)
                v.wait_ge(s_norm_st, 16 * TT)
                link(v.tensor_scalar(wide(0), wide(0), -80.0, 80.0, ALU.max, ALU.min))
                link(v.tensor_scalar(wide(1), wide(0), -LOG2E, MAGIC, ALU.mult, ALU.add))
                link(v.tensor_scalar(wide(1), wide(1), MAGIC, None, ALU.subtract))
                link(v.scalar_tensor_tensor(wide(2), wide(1), -LN2_HI, wide(0), ALU.mult, ALU.subtract))
                link(v.scalar_tensor_tensor(wide(2), wide(1), -LN2_LO, wide(2), ALU.mult, ALU.add))
                link(v.tensor_scalar(wide(3), wide(2), EXP_C[-1], None, ALU.mult))

            def scores_2():
                for coef in EXP_C[-2::-1]:
                    link(v.scalar_tensor_tensor(wide(3), wide(3), coef, wide(2), ALU.add, ALU.mult))
                link(v.tensor_scalar(wide(4).bitcast(I32), wide(1), 127.0, 2.0 ** 23, ALU.add, ALU.mult))

            def scores_3():
                link(v.scalar_tensor_tensor(wide(3), wide(3), 1.0, wide(4), ALU.add, ALU.mult))
                link(v.tensor_scalar(wide(3), wide(3), 1.0, None, ALU.add))
                link(v.reciprocal(wide(0), wide(3)))

            def groups_1():
                link(v.tensor_tensor(tte(1), tte(0), bias[:].unsqueeze(1).to_broadcast([P, TT, E]), ALU.add))
                col = lambda m: four[:, :, m]
                v.tensor_tensor(q4(2, 0), col(0), col(1), ALU.max)
                v.tensor_tensor(q4(2, 1), col(0), col(1), ALU.min)
                v.tensor_tensor(q4(2, 2), col(2), col(3), ALU.max)
                link(v.tensor_tensor(q4(2, 3), col(2), col(3), ALU.min))
                v.tensor_tensor(q4(3, 0), q4(2, 0), q4(2, 2), ALU.max)
                v.tensor_tensor(q4(3, 1), q4(2, 0), q4(2, 2), ALU.min)
                link(v.tensor_tensor(q4(3, 2), q4(2, 1), q4(2, 3), ALU.max))
                link(v.tensor_tensor(q4(3, 1), q4(3, 1), q4(3, 2), ALU.max))
                link(v.tensor_tensor(q4(2, 3), q4(3, 0), q4(3, 1), ALU.add))
                link(v.memset(scr[:, 3:5, :], 0.0))

            def groups_2():
                gs = q4(2, 3).rearrange("p (i g) -> p i g", g=G)
                pairs = scr[:, 3:5, :].rearrange("p a (i g o) -> p (a i) g o", g=G, o=G)
                for o in range(G):
                    if o > 0:
                        last = v.tensor_tensor(pairs[:, :, 0:o, o], gs[:, :, o].unsqueeze(2).to_broadcast([P, TT, o]), gs[:, :, 0:o], ALU.is_gt)
                    if o < G - 1:
                        last = v.tensor_tensor(pairs[:, :, o + 1:G, o], gs[:, :, o].unsqueeze(2).to_broadcast([P, TT, G - 1 - o]), gs[:, :, o + 1:G], ALU.is_ge)
                link(last)
                link(v.tensor_reduce(q4(2, 0), pairs, AX_X, ALU.add))
                link(v.tensor_scalar(q4(2, 1), q4(2, 0), TOPG - 0.5, None, ALU.is_lt))

            def groups_3():
                keep = q4(2, 1).unsqueeze(2).to_broadcast([P, TT * G, EG])
                link(v.tensor_tensor(wide(3).rearrange("p (q m) -> p q m", m=EG), four, keep, ALU.mult))
                link(v.tensor_scalar(wide(3), wide(3), 0.0, None, ALU.add))

            def largest(first, n):
                before = chain[1] + chain[2]
                with v.Fori(0, n) as i:
                    start(s_dve, i * 4 + before)
                    at = bass.ds(i * E + first * E, E)
                    link(v.tensor_copy(pick[:, 0, :], wide(3)[:, at]))
                    v.sem_inc(s_passed)
                    link(v.max(top8[:], pick[:, 0, :]))
                    v.sem_inc(s_passed)
                    link(v.match_replace(pick[:, 1, :], top8[:], pick[:, 0, :], TAKEN))
                    link(v.tensor_scalar(wide(4)[:, at], pick[:, 1, :], TAKEN, None, ALU.is_equal))
                start(s_dve, before + 4 * n)

            def weights():
                v.tensor_copy(sel_e.rearrange("p (e i) -> p e i", i=TT), tte(4).rearrange("p i e -> p e i")).then_inc(s_sel, 1)
                link(v.tensor_tensor(wide(1), wide(0), wide(4), ALU.mult))
                link(v.tensor_reduce(ef[:, 0, :], tte(1), AX_X, ALU.add))
                link(v.reciprocal(ef[:, 1, :], ef[:, 0, :]))
                link(v.tensor_tensor(tte(1), tte(1), ef[:, 1, :].unsqueeze(2).to_broadcast([P, TT, E]), ALU.mult))
                link(v.tensor_scalar(wide(1), wide(1), ROUTED_SCALE, None, ALU.mult))
                link(v.memset(wide(3), 1.0))
                link(v.memset(tte(3)[:, :, 0:1], 0.0))

            def counts():
                v.wait_ge(s_count, 4)
                for c in range(2):
                    last = v.tensor_copy(wide(2)[:, 512 * c:512 * c + 512], bank[4 + c][:])
                link(last)
                for c in range(2):
                    last = v.tensor_tensor(wide(0)[:, 512 * c:512 * c + 512], bank[2 + c][:], wide(2)[:, 512 * c:512 * c + 512], ALU.subtract)
                last.then_inc(s_counted, 1)
                v.wait_ge(s_counted, 1)

            def places_1():
                link(v.tensor_tensor_scan(wide(2), wide(3), wide(2), 0.0, ALU.mult, ALU.add))
                link(v.tensor_scalar(ei[:], eti(2)[:, :, TT - 1], float(P - 1), None, ALU.add))
                link(v.tensor_scalar(ei[:], ei[:], 7, None, ALU.logical_shift_right))
                link(v.tensor_scalar(ef[:, 2, :], ei[:], 1.0, None, ALU.max))
                link(v.memset(ef[:, 3, :], 1.0))
                link(v.tensor_tensor_scan(ef[:, 4, :], ef[:, 3, :], ef[:, 2, :], 0.0, ALU.mult, ALU.add))
                link(v.tensor_tensor(ef[:, 5, :], ef[:, 4, :], ef[:, 2, :], ALU.subtract))
                link(v.tensor_scalar(ef[:, 6, :], ef[:, 5, :], float(SHT), float(P), ALU.add, ALU.mult))
                link(v.tensor_scalar(ef[:, 7, :], ef[:, 4, :], float(SHT), None, ALU.add))
                link(v.tensor_scalar(pairs_i[:], ef[:, 7, E - 1:E], 1.0, None, ALU.add))
                link(v.tensor_scalar(pairs_i[:], pairs_i[:], 1, None, ALU.logical_shift_right))

            def places_2():
                link(v.tensor_tensor(wide(0), wide(0), wide(2), ALU.add))
                link(v.tensor_tensor(eti(0), eti(0), ef[:, 6, :].unsqueeze(2).to_broadcast([P, E, TT]), ALU.add))
                link(v.tensor_tensor_scan(wide(2), wide(3), wide(4), 0.0, ALU.mult, ALU.add))
                link(v.tensor_tensor(wide(2), wide(2), wide(4), ALU.mult))

            def numbered(ks):
                place = eti(0).rearrange("p e i -> p i e")
                picks_w = picks.bitcast(F32).rearrange("p (i k) two -> p i k two", k=TOPK)
                for k in ks:
                    link(v.scalar_tensor_tensor(tte(3), tte(2), float(k + 1), place, ALU.is_equal, ALU.mult))
                    link(v.tensor_reduce(slot_f[:, :, k], tte(3), AX_X, ALU.add))
                    link(v.scalar_tensor_tensor(tte(3), tte(2), float(k + 1), tte(1), ALU.is_equal, ALU.mult))
                    link(v.tensor_reduce(picks_w[:, :, k, 1], tte(3), AX_X, ALU.add))

            def tables():
                tok = token_no[:].unsqueeze(2).to_broadcast([P, TT, TOPK])
                v.tensor_copy(picks.rearrange("p (i k) two -> p i k two", k=TOPK)[:, :, :, 0], tok)
                link(v.tensor_copy(slot_i[:, 0, :], slot_f.rearrange("p i k -> p (i k)")))
                link(v.tensor_scalar(slot_i[:, 1, :], slot_i[:, 0, :], 7, None, ALU.logical_shift_right))
                link(v.tensor_scalar(slot_i[:, 0, :], slot_i[:, 0, :], P - 1, None, ALU.bitwise_and))
                v.scalar_tensor_tensor(slot_rows[:], slot_i[:, 0, :], float(LT), slot_i[:, 1, :], ALU.mult, ALU.add).then_inc(s_slots, 1)
                v.tensor_copy(tile_f[:, 0, :], tile_no[:])
                link(v.tensor_scalar(tile_f[:, 1, :], tile_no[:], 1.0, None, ALU.add))
                cmp = lambda d: wide(2 + d)[:, 0:3 * E].rearrange("p (c e) -> p c e", e=E)
                ends = ef[:, 7, :].unsqueeze(1).to_broadcast([P, 3, E])
                for d in range(2):
                    link(v.tensor_tensor(cmp(d), tile_f[:, d, :].unsqueeze(2).to_broadcast([P, 3, E]), ends, ALU.is_ge))
                    link(v.tensor_reduce(tile_c[:, d, :], cmp(d), AX_X, ALU.add))
                    link(v.scalar_tensor_tensor(tile_c[:, d, :], tile_f[:, d, :], float(TT), tile_c[:, d, :], ALU.is_ge, ALU.add))
                    link(v.scalar_tensor_tensor(tile_c[:, d, :], tile_f[:, d, :], float(SHT), tile_c[:, d, :], ALU.is_ge, ALU.add))
                    link(v.tensor_scalar(tile_c[:, d, :], tile_c[:, d, :], float(NE - 1), None, ALU.min))
                v.tensor_copy(set_i[:, 0, :], tile_c[:, 0, :])
                v.tensor_tensor(set_i[:, 1, :], tile_c[:, 1, :], tile_c[:, 0, :], ALU.subtract).then_inc(s_sets, 1)

            gathered_lo(0)
            scores_1()
            for c in (1, 2):
                split_lo(c, range(PARTS), 0)
            groups = TT // 8
            tile(0, 0)
            scores_2()
            tile(0, 1)
            scores_3()
            tile(0, 2)
            groups_1()
            tile(0, 3)
            groups_2()
            tile(0, 4)
            groups_3()
            for f in range(8):
                tile(0, 5 + f)
                largest(f * groups, groups)
            tile(0, COUNT_TILE - 1)
            weights()
            tile(0, COUNT_TILE)
            counts()
            places_1()
            tile(0, COUNT_TILE + 1)
            places_2()
            for k in range(0, TOPK, 2):
                tile(0, COUNT_TILE + 2 + k // 2)
                numbered((k, k + 1))
            tile(0, ROUTE_STEPS)
            tables()
            tile(0, ROUTE_STEPS + 1)
            with v.Fori(ROUTE_STEPS // 2 + 1, SHT // 2) as it:
                for n in range(2):
                    tile(it, n)
            v.wait_ge(s_meta, 16)
            pairs = v.value_load(pairs_i[0:1, 0:1], min_val=SHT // 2 + 1, max_val=NT // 2)
            with v.Fori(SHT // 2, NT // 2) as it:
                with v.If(it < pairs):
                    for n in range(2):
                        tile(it, n)

        @block.tensor
        def _(pe):
            def transposes(dst, src, c, done):
                for k in range(4):
                    last = pe.transpose(dst[:, k * P:(k + 1) * P], src[:, (4 * c + k) * P:(4 * c + k + 1) * P], ident[:])
                last.then_inc(done, 1)

            def products(dst, xs, ws, first, last):
                pe.matmul(dst, xs[0], ws[0], start=first, stop=False)
                pe.matmul(dst, xs[0], ws[1], start=False, stop=False)
                return pe.matmul(dst, xs[1], ws[0], start=False, stop=last)

            pe.wait_ge(s_const, 18)
            pe.wait_ge(s_rw, 32)
            def pe_step(t):
                z = t.lag(1)
                if z.real():
                    pe.wait_ge(s_back, z.count(1, 1))
                    after(pe, s_qlo, z.count(2))
                    for c in range(2):
                        transposes(bank[c], quot[z.n], c, s_qT)
                y = t.lag(3)
                if y.real():
                    pe.wait_ge(s_norm, y.count(1, 1))
                    after(pe, s_nTs, y.count(2))
                    for c in range(2):
                        transposes(bank[2 + c], wide(1), c, s_nT)
                y = t.lag(4)
                if y.real():
                    pe.wait_ge(s_nTs, y.count(2, 2))
                    after(pe, s_logit_s, y.count(1))
                    for k in range(KB):
                        last = pe.matmul(bank[4][:, 0:E], wide(2)[:, k * P:(k + 1) * P], rw[:, k, :], start=k == 0, stop=k == KB - 1)
                    last.then_inc(s_logit, 1)
                if z.real():
                    pe.wait_ge(s_qlo, z.count(2, 2))
                    after(pe, s_x1, z.count(1))
                for h in range(2):
                    if z.real():
                        cols = slice(512 * h, 512 * h + 512)
                        for k in range(KB):
                            pe.wait_ge(s_clo, z.batch(2 * KB, KB * h + k + 1))
                            last = products(bank[6 + h][:], (xT_hi[:, k, :], xT_lo[:, k, :]),
                                            (ctxT_hi[:, k, cols], ctxT_lo[:, k, cols]), k == 0, k == KB - 1)
                        last.then_inc(s_prod, 1)
                    c = t.next_batch().lag(1)
                    if h == 0 and c.real():
                        pe.wait_ge(s_cround, c.count(1, 1))
                        after(pe, s_cqT, c.count(1))
                        for k in range(KB):
                            last = pe.transpose(bank[5][:].bitcast(BF16)[:, k * P:(k + 1) * P], cq[:, k * P:(k + 1) * P], ident_b[:])
                        last.then_inc(s_cT, 1)

            phase_a(pe, pe_step)

            def count_picks():
                pe.wait_ge(s_sel, 1)
                pe.wait_ge(s_hlo, 2 * COUNT_TILE + 2)
                for n, m in ((2, tri), (4, ones)):
                    for c in range(2):
                        pe.matmul(bank[n + c][:], m[:], sel_e[:, 512 * c:512 * c + 512], start=True, stop=True).then_inc(s_count, 1)
                pe.wait_ge(s_counted, 1)

            def gathered(n, k, rows):
                pe.wait_ge(s_gath[n], rows)
                for c in range(2):
                    transposes(bank[c], row_in_t[n], c, s_xT)

            w_of = lambda c, n: tuple(w[:, c, :].rearrange("p (k n) -> p k n", n=n) for w in (w_hi, w_lo))
            pe.wait_ge(s_qlo, 2 * TT)
            gathered(0, 0, 16)

            def tile(it, n):
                t = it * 2 + n
                set_no = pe.value_load(tile_row[0:1, 0, bass.ds(t, 1)], min_val=0, max_val=NE - 1)
                pe.wait_ge(s_xlo, t * 2 + 2)
                pe.wait_ge(s_wlo, set_no * (3 * PARTS) + 1 * PARTS)
                hi, lo = w_of(0, I)
                for k in range(KB):
                    last = products(bank[2][:], (xT_hi[:, k, :], xT_lo[:, k, :]), (hi[:, k, :], lo[:, k, :]), k == 0, k == KB - 1)
                last.then_inc(s_gate, 1)
                pe.wait_ge(s_wlo, set_no * (3 * PARTS) + 2 * PARTS)
                hi, lo = w_of(1, I)

                def hidden(u):
                    pe.wait_ge(s_h, t * 2 + (u + 1))
                    pe.wait_ge(s_hlo, t * 2 + u)
                    for m in range(2):
                        last = pe.transpose(bank[5][:, m * P:(m + 1) * P], hid[:, (2 * u + m) * P:(2 * u + m + 1) * P], ident[:])
                    last.then_inc(s_hT, 1)

                for u in range(2):
                    cols = slice(256 * u, 256 * u + 256)
                    for k in range(KB):
                        if u == 1 and k == KB - 2:
                            hidden(0)
                        last = products(bank[3 + u][:, 0:256], (xT_hi[:, k, :], xT_lo[:, k, :]),
                                        (hi[:, k, cols], lo[:, k, cols]), k == 0, k == KB - 1)
                    last.then_inc(s_up, 1)
                gathered(1 - n, t + 1, it * 16 + (16 + 16 * n))
                hidden(1)
                pe.wait_ge(s_wlo, set_no * (3 * PARTS) + 3 * PARTS)
                pe.wait_ge(s_y, t * 2)
                hi, lo = w_of(2, H)
                for u in range(2):
                    pe.wait_ge(s_hlo, t * 2 + (u + 1))
                    for h in range(2):
                        cols = slice(512 * h, 512 * h + 512)
                        for m in (2 * u, 2 * u + 1):
                            last = products(bank[6 + h][:], (hT_hi[:, m, :], hT_lo[:, m, :]),
                                            (hi[:, m, cols], lo[:, m, cols]), m == 0, m == IB - 1)
                        if u == 1:
                            last.then_inc(s_down, 1)

            with pe.Fori(0, COUNT_PAIR) as it:
                for n in range(2):
                    tile(it, n)
            tile(COUNT_PAIR, 0)
            count_picks()
            tile(COUNT_PAIR, 1)
            with pe.Fori(COUNT_PAIR + 1, SHT // 2) as it:
                for n in range(2):
                    tile(it, n)
            pe.wait_ge(s_meta, 16)
            pairs = pe.value_load(pairs_i[0:1, 0:1], min_val=SHT // 2 + 1, max_val=NT // 2)
            with pe.Fori(SHT // 2, NT // 2) as it:
                with pe.If(it < pairs):
                    for n in range(2):
                        tile(it, n)


_INS = ['x', 'ctx_2048', 'L0_ffn_router_w', 'L0_ffn_router_bias', 'L0_ffn_w_gate', 'L0_ffn_w_up', 'L0_ffn_w_down',
        'L0_ffn_sw_gate', 'L0_ffn_sw_up', 'L0_ffn_sw_down']


def kernel(**inputs):
    import numpy as _np
    import concourse.bacc as _bacc
    from concourse import mybir as _mybir
    from concourse.bass_utils import run_bass_kernel_spmd as _run

    nc = _bacc.Bacc("TRN2", target_bir_lowering=False, num_devices=1)
    arrays, args = {}, []
    for name in _INS:
        a = _np.ascontiguousarray(inputs[name])
        arrays[f"in_{name}_dram"] = a
        args.append(nc.dram_tensor(f"in_{name}_dram", a.shape, _mybir.dt.from_np(a.dtype), kind="ExternalInput").ap())
    args.append(nc.dram_tensor("out_0_dram", (T + P, H), F32, kind="ExternalOutput").ap())
    xattn_moe_program(nc, *args)
    r = _run(nc, [arrays], core_ids=[0])
    return r.results[0]["out_0_dram"][:T].reshape(B, S, H)
```
